# Optimizing a Trainium2 kernel written in Bass

```python
import numpy as np
import jax
import jax.numpy as jnp

def _softmax(x, axis=-1):
    return jax.nn.softmax(x, axis=axis)

def _gelu(x):
    return jax.nn.gelu(x, approximate=True)

def _silu(x):
    return jax.nn.silu(x)

def _sigmoid(x):
    return jax.nn.sigmoid(x)

def _layernorm(x, axis=-1, eps=1e-05):
    m = jnp.mean(x, axis=axis, keepdims=True)
    v = jnp.var(x, axis=axis, keepdims=True)
    return (x - m) / jnp.sqrt(v + eps)

def _scatter_add(tgt, idx, src, axis=0):
    return tgt.at[idx].add(src)

def _segment_sum(src, seg, n):
    return jax.ops.segment_sum(src, seg, n)
kernel_name = 'mk_flamingo_gated_d2_seqx_r8_d5ea69'

def setup_inputs(seed: int=0):
    np.random.seed(seed)
    _w = jnp.asarray

    def _rec_inputs():
        import jax
        import jax.numpy as jnp
        _rk = jax.random.key(seed)
        x = -0.0002928 + 1 * jax.random.normal(jax.random.fold_in(_rk, 1), (64, 64, 128), jnp.float32)
        _lenS = 64 - jax.random.randint(jax.random.fold_in(_rk, 7), (64,), 0, max(1, 64 // 4) + 1, jnp.int32)
        _lenS2 = 64 - jax.random.randint(jax.random.fold_in(_rk, 8), (64,), 0, max(1, 64 // 4) + 1, jnp.int32)
        _ctx_1024P = jax.random.normal(jax.random.fold_in(_rk, 11), (64, 16, 128), jnp.float32)
        _ctx_1024c = jax.random.dirichlet(jax.random.fold_in(_rk, 511), 0.3 * jnp.ones((16,), jnp.float32), (64, 64))
        _ctx_1024t = jnp.einsum('bsk,bkd->bsd', _ctx_1024c, _ctx_1024P)
        _ctx_1024t = _ctx_1024t * jax.lax.rsqrt(jnp.mean(jnp.square(_ctx_1024t)) + 1e-12) * 0.953939
        ctx_1024 = -1.39393e-06 + 0.999914 * (_ctx_1024t + 0.3 * jax.random.normal(jax.random.fold_in(_rk, 611), (64, 64, 128), jnp.float32))
        _g = jax.random.normal(jax.random.fold_in(_rk, 9001), (2, 2), jnp.float32)
        _g = jnp.sign(_g) * jnp.maximum(jnp.abs(_g), 1.0) + (_g == 0) * 1.0
        g_xattn = _g[0]
        g_ffn = _g[1]
        return (x, ctx_1024, g_xattn, g_ffn)
    x, ctx_1024, g_xattn, g_ffn = _rec_inputs()

    def _L0_xattn_setup():
        import jax, jax.numpy as jnp
        import numpy as np
        H, DK, DV = (16, 64, 64)
        MEM = 128
        D_MODEL = 128
        OUT_DIM = 128
        key = jax.random.key(seed)
        ks = jax.random.split(key, 12)
        B, S = (2, 256)
        scale = 1.0 / np.sqrt(D_MODEL)
        inp = {'queries': jax.random.normal(ks[0], (B, S, D_MODEL), jnp.float32), 'keys': jax.random.normal(ks[1], (B, S, D_MODEL), jnp.float32), 'values': jax.random.normal(ks[2], (B, S, D_MODEL), jnp.float32), 'wq_w': jax.random.normal(ks[3], (D_MODEL, H * DK), jnp.float32) * scale, 'wq_b': jnp.zeros((H * DK,), jnp.float32), 'wk_w': jax.random.normal(ks[4], (D_MODEL, H * DK), jnp.float32) * scale, 'wk_b': jnp.zeros((H * DK,), jnp.float32), 'wv_w': jax.random.normal(ks[5], (D_MODEL, H * DV), jnp.float32) * scale, 'wv_b': jnp.zeros((H * DV,), jnp.float32), 'mk': jax.random.normal(ks[6], (1, MEM, H * DK), jnp.float32) * (0.1 / DK), 'mv': jax.random.normal(ks[7], (1, MEM, H * DV), jnp.float32) * (0.1 / MEM), 'wo_w': jax.random.normal(ks[8], (H * DV, OUT_DIM), jnp.float32) * (1.0 / np.sqrt(H * DV)), 'wo_b': jnp.zeros((OUT_DIM,), jnp.float32)}
        return inp
    _L0_xattn_all = _L0_xattn_setup()
    _L0_xattn_in = {k: v for k, v in _L0_xattn_all.items() if k in ('wq_w', 'wq_b', 'wk_w', 'wk_b', 'wv_w', 'wv_b', 'mk', 'mv', 'wo_w', 'wo_b')}
    del _L0_xattn_all

    def _L0_ffn_setup():
        import jax, jax.numpy as jnp
        import numpy as np
        DIM = 128
        DEPTH = 6
        HEADS = 16
        DIM_HEAD = 64
        WINDOW = 32
        INNER = HEADS * DIM_HEAD
        DIM_INNER = int(DIM * 4 * 2 / 3)
        QK_SCALE = 8.0

        def shift_tokens(t):
            a, s = jnp.split(t, 2, -1)
            s = jnp.pad(s, ((0, 0), (1, 0), (0, 0)))[:, :-1]
            return jnp.concatenate([a, s], -1)

        def l2norm(t):
            return t / jnp.maximum(jnp.linalg.norm(t, axis=-1, keepdims=True), 1e-12)

        def rotate_half(x):
            x1, x2 = jnp.split(x, 2, -1)
            return jnp.concatenate([-x2, x1], -1)

        def rotary_tables(n):
            half = jnp.arange(0, DIM_HEAD, 2, dtype=jnp.float32)
            inv_freq = 1.0 / 10000.0 ** (half / DIM_HEAD)
            t = jnp.arange(n, dtype=jnp.float32)
            freqs = t[:, None] * inv_freq[None, :]
            freqs = jnp.concatenate([freqs, freqs], -1)
            base_scale = (half + 0.4 * DIM_HEAD) / (1.4 * DIM_HEAD)
            power = (t - n // 2) / (WINDOW // 2)
            scale = base_scale[None, :] ** power[:, None]
            scale = jnp.concatenate([scale, scale], -1)
            return (freqs, scale)

        def local_attention(q, k, v):
            b, h, n, d = q.shape
            w = WINDOW
            nw = n // w
            bq = q.reshape(b, h, nw, w, d)
            bk = k.reshape(b, h, nw, w, d)
            bv = v.reshape(b, h, nw, w, d)

            def look(t):
                p = jnp.pad(t, ((0, 0), (0, 0), (1, 0), (0, 0), (0, 0)))
                return jnp.concatenate([p[:, :, :nw], p[:, :, 1:]], axis=3)
            bk2, bv2 = (look(bk), look(bv))
            seq = jnp.arange(n).reshape(nw, w)
            seq_p = jnp.pad(seq, ((1, 0), (0, 0)), constant_values=-1)
            jt = jnp.concatenate([seq_p[:nw], seq_p[1:]], axis=1)
            it = seq[:, :, None]
            jb = jt[:, None, :]
            mask = (it < jb) | (it > jb + w) | (jb == -1)
            sim = jnp.einsum('bhwie,bhwje->bhwij', bq, bk2) * QK_SCALE
            sim = jnp.where(mask, -jnp.finfo(sim.dtype).max, sim)
            attn = jax.nn.softmax(sim, -1)
            out = jnp.einsum('bhwij,bhwje->bhwie', attn, bv2)
            return out.reshape(b, h, n, d)

        def attn_layer(x, Wqkv, qs, ksc, Wo):
            b, n, _ = x.shape
            qkv = x @ Wqkv
            q, k, v = jnp.split(qkv, 3, -1)
            sh = lambda t: t.reshape(b, n, HEADS, DIM_HEAD).transpose(0, 2, 1, 3)
            q, k, v = (sh(q), sh(k), sh(v))
            q = l2norm(q) * qs
            k = l2norm(k) * ksc
            freqs, scale = rotary_tables(n)
            cos, sin = (jnp.cos(freqs), jnp.sin(freqs))
            q = q * cos * scale + rotate_half(q) * sin * scale
            inv = 1.0 / scale
            k = k * cos * inv + rotate_half(k) * sin * inv
            out = local_attention(q, k, v)
            out = out.transpose(0, 2, 1, 3).reshape(b, n, INNER)
            return out @ Wo

        def ffn_layer(x, g, bln, W1, b1, W2, b2):
            mu = x.mean(-1, keepdims=True)
            var = ((x - mu) ** 2).mean(-1, keepdims=True)
            xn = (x - mu) / jnp.sqrt(var + 1e-05) * g + bln
            hg = xn @ W1 + b1
            a, gate = jnp.split(hg, 2, -1)
            return a * jax.nn.gelu(gate, approximate=False) @ W2 + b2
        key = jax.random.key(seed)
        ks = jax.random.split(key, 8)
        B, N = (2, 256)
        init = lambda k, shape: jax.random.normal(k, shape, jnp.float32) * 0.02
        return {'x': jax.random.normal(ks[0], (B, N, DIM), jnp.float32), 'Wqkv': init(ks[1], (DEPTH, DIM, 3 * INNER)), 'q_scale': jnp.ones((DEPTH, DIM_HEAD), jnp.float32), 'k_scale': jnp.ones((DEPTH, DIM_HEAD), jnp.float32), 'Wo': init(ks[2], (DEPTH, INNER, DIM)), 'ln_g': jnp.ones((DEPTH, DIM), jnp.float32), 'ln_b': jnp.zeros((DEPTH, DIM), jnp.float32), 'W1': init(ks[3], (DEPTH, DIM, 2 * DIM_INNER)), 'b1': jnp.zeros((DEPTH, 2 * DIM_INNER), jnp.float32), 'W2': init(ks[4], (DEPTH, DIM_INNER, DIM)), 'b2': jnp.zeros((DEPTH, DIM), jnp.float32)}
    _L0_ffn_all = _L0_ffn_setup()
    _L0_ffn_in = {k: v for k, v in _L0_ffn_all.items() if k in ('Wqkv', 'q_scale', 'k_scale', 'Wo', 'ln_g', 'ln_b', 'W1', 'b1', 'W2', 'b2')}
    del _L0_ffn_all

    def _L1_xattn_setup():
        import jax, jax.numpy as jnp
        import numpy as np
        DIM = 128
        HEADS = 16
        HEAD_DIM = DIM // HEADS
        SCALE = HEAD_DIM ** (-0.5)
        key = jax.random.key(seed)
        ks = jax.random.split(key, 8)
        B, Nx, N, C = (4, 256, 64, DIM)
        s = C ** (-0.5)
        return {'x': jax.random.normal(ks[0], (B, Nx, C), jnp.float32), 'cls': jax.random.normal(ks[1], (B, N, C), jnp.float32), 'w_kv': jax.random.normal(ks[2], (C, 2 * C), jnp.float32) * s, 'w_q': jax.random.normal(ks[3], (C, C), jnp.float32) * s, 'w_la': jax.random.normal(ks[4], (C, HEADS), jnp.float32) * s, 'w_proj': jax.random.normal(ks[5], (C, C), jnp.float32) * s, 'b_proj': jax.random.normal(ks[6], (C,), jnp.float32) * 0.01, 'att_weight': jax.random.normal(ks[7], (1,), jnp.float32) * 0.1}
    _L1_xattn_all = _L1_xattn_setup()
    _L1_xattn_in = {k: v for k, v in _L1_xattn_all.items() if k in ('w_kv', 'w_q', 'w_la', 'w_proj', 'b_proj', 'att_weight')}
    del _L1_xattn_all

    def _L1_ffn_setup():
        import jax, jax.numpy as jnp
        import numpy as np
        DIM = 128
        INTER = 128
        N_EXPERTS = 8
        TOPK = 2
        N_SHARED = 2
        key = jax.random.key(seed)
        ks = jax.random.split(key, 10)
        s = 0.02
        return {'x': jax.random.normal(ks[0], (4, 256, DIM), dtype=jnp.float32), 'gate_w': jax.random.normal(ks[1], (N_EXPERTS, DIM), dtype=jnp.float32) * s, 'gate_bias': jax.random.normal(ks[2], (N_EXPERTS,), dtype=jnp.float32) * s, 'w1': jax.random.normal(ks[3], (N_EXPERTS, INTER, DIM), dtype=jnp.float32) * s, 'w3': jax.random.normal(ks[4], (N_EXPERTS, INTER, DIM), dtype=jnp.float32) * s, 'w2': jax.random.normal(ks[5], (N_EXPERTS, DIM, INTER), dtype=jnp.float32) * s, 'sw1': jax.random.normal(ks[6], (N_SHARED * INTER, DIM), dtype=jnp.float32) * s, 'sw3': jax.random.normal(ks[7], (N_SHARED * INTER, DIM), dtype=jnp.float32) * s, 'sw2': jax.random.normal(ks[8], (DIM, N_SHARED * INTER), dtype=jnp.float32) * s}
    _L1_ffn_all = _L1_ffn_setup()
    _L1_ffn_in = {k: v for k, v in _L1_ffn_all.items() if k in ('gate_w', 'gate_bias', 'w1', 'w3', 'w2', 'sw1', 'sw3', 'sw2')}
    del _L1_ffn_all
    return {'x': x, 'ctx_1024': ctx_1024, 'g_xattn': g_xattn, 'g_ffn': g_ffn, 'L0_xattn_wq_w': _L0_xattn_in['wq_w'], 'L0_xattn_wq_b': _L0_xattn_in['wq_b'], 'L0_xattn_wk_w': _L0_xattn_in['wk_w'], 'L0_xattn_wk_b': _L0_xattn_in['wk_b'], 'L0_xattn_wv_w': _L0_xattn_in['wv_w'], 'L0_xattn_wv_b': _L0_xattn_in['wv_b'], 'L0_xattn_mk': _L0_xattn_in['mk'], 'L0_xattn_mv': _L0_xattn_in['mv'], 'L0_xattn_wo_w': _L0_xattn_in['wo_w'], 'L0_xattn_wo_b': _L0_xattn_in['wo_b'], 'L0_ffn_Wqkv': _L0_ffn_in['Wqkv'], 'L0_ffn_q_scale': _L0_ffn_in['q_scale'], 'L0_ffn_k_scale': _L0_ffn_in['k_scale'], 'L0_ffn_Wo': _L0_ffn_in['Wo'], 'L0_ffn_ln_g': _L0_ffn_in['ln_g'], 'L0_ffn_ln_b': _L0_ffn_in['ln_b'], 'L0_ffn_W1': _L0_ffn_in['W1'], 'L0_ffn_b1': _L0_ffn_in['b1'], 'L0_ffn_W2': _L0_ffn_in['W2'], 'L0_ffn_b2': _L0_ffn_in['b2'], 'L1_xattn_w_kv': _L1_xattn_in['w_kv'], 'L1_xattn_w_q': _L1_xattn_in['w_q'], 'L1_xattn_w_la': _L1_xattn_in['w_la'], 'L1_xattn_w_proj': _L1_xattn_in['w_proj'], 'L1_xattn_b_proj': _L1_xattn_in['b_proj'], 'L1_xattn_att_weight': _L1_xattn_in['att_weight'], 'L1_ffn_gate_w': _L1_ffn_in['gate_w'], 'L1_ffn_gate_bias': _L1_ffn_in['gate_bias'], 'L1_ffn_w1': _L1_ffn_in['w1'], 'L1_ffn_w3': _L1_ffn_in['w3'], 'L1_ffn_w2': _L1_ffn_in['w2'], 'L1_ffn_sw1': _L1_ffn_in['sw1'], 'L1_ffn_sw3': _L1_ffn_in['sw3'], 'L1_ffn_sw2': _L1_ffn_in['sw2']}

def reference(x, ctx_1024, g_xattn, g_ffn, L0_xattn_wq_w, L0_xattn_wq_b, L0_xattn_wk_w, L0_xattn_wk_b, L0_xattn_wv_w, L0_xattn_wv_b, L0_xattn_mk, L0_xattn_mv, L0_xattn_wo_w, L0_xattn_wo_b, L0_ffn_Wqkv, L0_ffn_q_scale, L0_ffn_k_scale, L0_ffn_Wo, L0_ffn_ln_g, L0_ffn_ln_b, L0_ffn_W1, L0_ffn_b1, L0_ffn_W2, L0_ffn_b2, L1_xattn_w_kv, L1_xattn_w_q, L1_xattn_w_la, L1_xattn_w_proj, L1_xattn_b_proj, L1_xattn_att_weight, L1_ffn_gate_w, L1_ffn_gate_bias, L1_ffn_w1, L1_ffn_w3, L1_ffn_w2, L1_ffn_sw1, L1_ffn_sw3, L1_ffn_sw2):
    import jax
    import jax.numpy as jnp

    def _L0_xattn_ref(queries, keys, values, wq_w, wq_b, wk_w, wk_b, wv_w, wv_b, mk, mv, wo_w, wo_b):
        import jax, jax.numpy as jnp
        import numpy as np
        H, DK, DV = (16, 64, 64)
        MEM = 128
        D_MODEL = 128
        OUT_DIM = 128
        B, S, _ = queries.shape
        q = (queries @ wq_w + wq_b).reshape(B, S, H, DK).transpose(0, 2, 1, 3)
        k_proj = keys @ wk_w + wk_b
        v_proj = values @ wv_w + wv_b
        k_ext = jnp.concatenate([k_proj, jnp.broadcast_to(mk, (B, MEM, H * DK))], axis=1)
        v_ext = jnp.concatenate([v_proj, jnp.broadcast_to(mv, (B, MEM, H * DV))], axis=1)
        T = S + MEM
        k = k_ext.reshape(B, T, H, DK).transpose(0, 2, 1, 3)
        v = v_ext.reshape(B, T, H, DV).transpose(0, 2, 1, 3)
        scores = jnp.einsum('bhsd,bhtd->bhst', q, k) / jnp.sqrt(jnp.float32(DK))
        attn = jax.nn.softmax(scores, axis=-1)
        out = jnp.einsum('bhst,bhtd->bhsd', attn, v)
        out = out.transpose(0, 2, 1, 3).reshape(B, S, H * DV)
        return out @ wo_w + wo_b

    def _L0_ffn_ref(x, Wqkv, q_scale, k_scale, Wo, ln_g, ln_b, W1, b1, W2, b2):
        import jax, jax.numpy as jnp
        import numpy as np
        DIM = 128
        DEPTH = 6
        HEADS = 16
        DIM_HEAD = 64
        WINDOW = 32
        INNER = HEADS * DIM_HEAD
        DIM_INNER = int(DIM * 4 * 2 / 3)
        QK_SCALE = 8.0

        def shift_tokens(t):
            a, s = jnp.split(t, 2, -1)
            s = jnp.pad(s, ((0, 0), (1, 0), (0, 0)))[:, :-1]
            return jnp.concatenate([a, s], -1)

        def l2norm(t):
            return t / jnp.maximum(jnp.linalg.norm(t, axis=-1, keepdims=True), 1e-12)

        def rotate_half(x):
            x1, x2 = jnp.split(x, 2, -1)
            return jnp.concatenate([-x2, x1], -1)

        def rotary_tables(n):
            half = jnp.arange(0, DIM_HEAD, 2, dtype=jnp.float32)
            inv_freq = 1.0 / 10000.0 ** (half / DIM_HEAD)
            t = jnp.arange(n, dtype=jnp.float32)
            freqs = t[:, None] * inv_freq[None, :]
            freqs = jnp.concatenate([freqs, freqs], -1)
            base_scale = (half + 0.4 * DIM_HEAD) / (1.4 * DIM_HEAD)
            power = (t - n // 2) / (WINDOW // 2)
            scale = base_scale[None, :] ** power[:, None]
            scale = jnp.concatenate([scale, scale], -1)
            return (freqs, scale)

        def local_attention(q, k, v):
            b, h, n, d = q.shape
            w = WINDOW
            nw = n // w
            bq = q.reshape(b, h, nw, w, d)
            bk = k.reshape(b, h, nw, w, d)
            bv = v.reshape(b, h, nw, w, d)

            def look(t):
                p = jnp.pad(t, ((0, 0), (0, 0), (1, 0), (0, 0), (0, 0)))
                return jnp.concatenate([p[:, :, :nw], p[:, :, 1:]], axis=3)
            bk2, bv2 = (look(bk), look(bv))
            seq = jnp.arange(n).reshape(nw, w)
            seq_p = jnp.pad(seq, ((1, 0), (0, 0)), constant_values=-1)
            jt = jnp.concatenate([seq_p[:nw], seq_p[1:]], axis=1)
            it = seq[:, :, None]
            jb = jt[:, None, :]
            mask = (it < jb) | (it > jb + w) | (jb == -1)
            sim = jnp.einsum('bhwie,bhwje->bhwij', bq, bk2) * QK_SCALE
            sim = jnp.where(mask, -jnp.finfo(sim.dtype).max, sim)
            attn = jax.nn.softmax(sim, -1)
            out = jnp.einsum('bhwij,bhwje->bhwie', attn, bv2)
            return out.reshape(b, h, n, d)

        def attn_layer(x, Wqkv, qs, ksc, Wo):
            b, n, _ = x.shape
            qkv = x @ Wqkv
            q, k, v = jnp.split(qkv, 3, -1)
            sh = lambda t: t.reshape(b, n, HEADS, DIM_HEAD).transpose(0, 2, 1, 3)
            q, k, v = (sh(q), sh(k), sh(v))
            q = l2norm(q) * qs
            k = l2norm(k) * ksc
            freqs, scale = rotary_tables(n)
            cos, sin = (jnp.cos(freqs), jnp.sin(freqs))
            q = q * cos * scale + rotate_half(q) * sin * scale
            inv = 1.0 / scale
            k = k * cos * inv + rotate_half(k) * sin * inv
            out = local_attention(q, k, v)
            out = out.transpose(0, 2, 1, 3).reshape(b, n, INNER)
            return out @ Wo

        def ffn_layer(x, g, bln, W1, b1, W2, b2):
            mu = x.mean(-1, keepdims=True)
            var = ((x - mu) ** 2).mean(-1, keepdims=True)
            xn = (x - mu) / jnp.sqrt(var + 1e-05) * g + bln
            hg = xn @ W1 + b1
            a, gate = jnp.split(hg, 2, -1)
            return a * jax.nn.gelu(gate, approximate=False) @ W2 + b2
        for i in range(DEPTH):
            x = attn_layer(shift_tokens(x), Wqkv[i], q_scale[i], k_scale[i], Wo[i]) + x
            x = ffn_layer(shift_tokens(x), ln_g[i], ln_b[i], W1[i], b1[i], W2[i], b2[i]) + x
        return x

    def _L1_xattn_ref(x, cls, w_kv, w_q, w_la, w_proj, b_proj, att_weight):
        import jax, jax.numpy as jnp
        import numpy as np
        DIM = 128
        HEADS = 16
        HEAD_DIM = DIM // HEADS
        SCALE = HEAD_DIM ** (-0.5)
        B, N, C = cls.shape
        Nx = x.shape[1]
        H, D = (HEADS, C // HEADS)
        kv = (x @ w_kv).reshape(B, Nx, 2, H, D)
        k = jnp.transpose(kv[:, :, 0], (0, 2, 1, 3))
        v = jnp.transpose(kv[:, :, 1], (0, 2, 1, 3))
        q = jnp.transpose((cls @ w_q).reshape(B, N, H, D), (0, 2, 1, 3))
        attn = jax.nn.softmax(jnp.einsum('bhnd,bhmd->bhnm', q, k) * SCALE, axis=-1)
        g = jnp.transpose(x @ w_la, (0, 2, 1))
        g_mean = jnp.mean(g, axis=-1)[:, :, None, None]
        g_max = jnp.max(g, axis=-1)[:, :, None, None]
        gate = 0.5 * g_mean + 0.5 * g_max
        attn2 = jax.nn.softmax(gate * attn, axis=-1)
        w = att_weight[0]
        attn = w * attn2 + (1.0 - w) * attn
        out = jnp.einsum('bhnm,bhmd->bnhd', attn, v).reshape(B, N, C)
        return out @ w_proj + b_proj

    def _L1_ffn_ref(x, gate_w, gate_bias, w1, w3, w2, sw1, sw3, sw2):
        import jax, jax.numpy as jnp
        import numpy as np
        DIM = 128
        INTER = 128
        N_EXPERTS = 8
        TOPK = 2
        N_SHARED = 2
        shape = x.shape
        xt = x.reshape(-1, shape[-1])
        scores = jax.nn.softmax((xt @ gate_w.T).astype(jnp.float32), axis=-1)
        _, idx = jax.lax.top_k(scores + gate_bias, TOPK)
        weights = jnp.take_along_axis(scores, idx, axis=1).astype(x.dtype)
        y = jnp.zeros_like(xt)
        for e in range(N_EXPERTS):
            gate_e = jnp.sum(jnp.where(idx == e, weights, 0.0), axis=1)
            h = jax.nn.silu(xt @ w1[e].T) * (xt @ w3[e].T)
            y = y + gate_e[:, None] * (h @ w2[e].T)
        z = jax.nn.silu(xt @ sw1.T) * (xt @ sw3.T) @ sw2.T
        return (y + z).reshape(shape)
    x = x + jnp.tanh(g_xattn[0]) * _L0_xattn_ref(_layernorm(x, axis=-1), ctx_1024, ctx_1024, L0_xattn_wq_w, L0_xattn_wq_b, L0_xattn_wk_w, L0_xattn_wk_b, L0_xattn_wv_w, L0_xattn_wv_b, L0_xattn_mk, L0_xattn_mv, L0_xattn_wo_w, L0_xattn_wo_b)
    x = x + jnp.tanh(g_ffn[0]) * _L0_ffn_ref(_layernorm(x, axis=-1), L0_ffn_Wqkv, L0_ffn_q_scale, L0_ffn_k_scale, L0_ffn_Wo, L0_ffn_ln_g, L0_ffn_ln_b, L0_ffn_W1, L0_ffn_b1, L0_ffn_W2, L0_ffn_b2)
    x = x + jnp.tanh(g_xattn[1]) * _L1_xattn_ref(ctx_1024, _layernorm(x, axis=-1), L1_xattn_w_kv, L1_xattn_w_q, L1_xattn_w_la, L1_xattn_w_proj, L1_xattn_b_proj, L1_xattn_att_weight)
    x = x + jnp.tanh(g_ffn[1]) * _L1_ffn_ref(_layernorm(x, axis=-1), L1_ffn_gate_w, L1_ffn_gate_bias, L1_ffn_w1, L1_ffn_w3, L1_ffn_w2, L1_ffn_sw1, L1_ffn_sw3, L1_ffn_sw2)
    return x

_drawn_inputs = setup_inputs


def setup_inputs(seed=0):
    import zlib

    import numpy as np

    out = dict(_drawn_inputs(seed))
    spreads = {'g_ffn': (-1.0, 0.6),
     'L0_xattn_wq_b': (0.0, 0.8),
     'L0_xattn_wk_b': (0.0, 0.8),
     'L0_xattn_wv_b': (0.0, 0.31),
     'L0_xattn_wo_b': (0.0, 0.1),
     'L0_ffn_q_scale': (1.0, 0.6),
     'L0_ffn_k_scale': (1.0, 0.6),
     'L0_ffn_ln_g': (1.0, 0.6),
     'L0_ffn_ln_b': (0.0, 0.8),
     'L0_ffn_b1': (0.0, 0.324),
     'L0_ffn_b2': (0.0, 0.1)}
    factors = {'L0_xattn_mk': 200.0,
     'L0_xattn_mv': 200.0,
     'L1_xattn_w_la': 200.0,
     'L1_xattn_b_proj': 3.632,
     'L1_ffn_gate_w': 8.0,
     'L1_ffn_gate_bias': 8.0,
     'L1_ffn_w1': 8.0,
     'L1_ffn_w3': 8.0,
     'L1_ffn_w2': 8.0,
     'L1_ffn_sw1': 5.339,
     'L1_ffn_sw3': 5.29,
     'L1_ffn_sw2': 5.304}
    for name, (base, spread) in spreads.items():
        noise = np.random.default_rng([zlib.crc32(name.encode()), seed]).standard_normal(out[name].shape)
        drawn = base * np.exp(spread * noise) if base else spread * noise
        out[name] = jnp.asarray(drawn.astype(out[name].dtype))
    for name, factor in factors.items():
        out[name] = (out[name] * factor).astype(out[name].dtype)
    return out
```

```python
from contextlib import ExitStack

import concourse.bass as bass
from concourse import mybir

P = 128
B, S, D = 64, 64, 128
BT = P // S
NT = B // BT
H, DK = 16, 64
HP = H // 2
INNER = H * DK
MEM = 128
DEPTH = 6
WINDOW = 32
FI = int(D * 4 * 2 / 3)
FBLK = [(0, P), (P, P), (2 * P, FI - 2 * P)]
FT = 2
NF = NT // FT
L1H, L1D = 16, 8
NE = 8
NEX = NE + 2
MT = 4
NM = NT // MT
QK_SCALE = 8.0
MASKED = -1e30
EPS = 1e-5

ALU = mybir.AluOpType
ACT = mybir.ActivationFunctionType
F32 = mybir.dt.float32
BF16 = mybir.dt.bfloat16
U32 = mybir.dt.uint32
AX = mybir.AxisListType.X

CONSTS = {}
_at = 0
for _name, _n in (("ident", P), ("shift", P), ("qcos", DK), ("kcos", DK), ("qsin", DK), ("ksin", DK),
                  ("band", DK), ("iota", NE), ("headmask", L1H), ("half", NT), ("eps", 4), ("ones", P)):
    CONSTS[_name] = (_at, _n)
    _at += _n
NCONST = _at


def build(nc, x, ctx, g_xattn, g_ffn, wq_w, wq_b, wk_w, wk_b, wv_w, wv_b, mk, mv, wo_w, wo_b,
          Wqkv, q_scale, k_scale, Wo, ln_g, ln_b, W1, b1, W2, b2,
          w_kv, w_q, w_la, w_proj, b_proj, att_weight,
          gate_w, gate_bias, w1, w3, w2, sw1, sw3, sw2, consts, out, stop=9):
    with ExitStack() as stack:
        def sb(name, shape, dt=F32):
            return stack.enter_context(nc.sbuf_tensor(name, shape, dt))

        sems = {}

        def sem(name):
            if name not in sems:
                sems[name] = stack.enter_context(nc.semaphore(name))
            return sems[name]

        X = sb("X", [P, NT, D])
        Y = sb("Y", [P, NT, D])
        CT = sb("CT", [P, NT, D])
        K = sb("K", [P, NCONST])

        def const(name):
            a, n = CONSTS[name]
            return K[:, a:a + n]

        ident = const("ident")
        identb = sb("identb", [P, P], BF16)
        bandb = sb("bandb", [P, 4, BT, S], BF16)
        gates = sb("gates", [P, 4])
        tg = sb("tg", [P, 4])
        st = sb("st", [P, NT, 6])
        mean = sb("mean", [P, NT])
        dif = sb("dif", [P, NT])
        var = sb("var", [P, NT])
        m2 = sb("m2", [P, NT])
        rstd = sb("rstd", [P, NT])
        nhalf = const("half")

        xq = sb("xq", [P, INNER])
        xk = sb("xk", [P, INNER])
        xv = sb("xv", [P, INNER])
        xo = sb("xo", [P, HP, D])
        mkn = sb("mkn", [P, INNER])
        mkT = sb("mkT", [P, HP, MEM])
        mvn = sb("mvn", [P, INNER])
        qb = sb("qb", [P, HP])
        kb = sb("kb", [P, HP])
        vb = sb("vb", [P, HP, DK])
        ob = sb("ob", [P, D])
        wqkv = sb("wqkv", [P, 3 * INNER])
        wo = sb("wo", [P, HP, D])
        qs = sb("qs", [P, 2, DK])
        rc_ = sb("ropec", [P, 2, DK])
        rs_ = sb("ropes", [P, 2, DK])
        fw1 = sb("fw1", [P, 2 * FI])
        fw2 = sb("fw2", [P, 3, D])
        fg = sb("fg", [P, 2])
        fb1 = sb("fb1", [P, 2, 3])
        fb2 = sb("fb2", [1, D])
        lkv = sb("lkv", [P, 2 * D])
        lq = sb("lq", [P, D])
        lla = sb("lla", [P, L1H])
        lpj = sb("lpj", [P, D])
        lpb = sb("lpb", [P, D])
        law = sb("law", [P, 2])
        egw = sb("egw", [NE, D])
        egT = sb("egT", [P, NE])
        egb = sb("egb", [P, NE])
        G = sb("G", [P, NT, NE])

        xs = sb("xs", [P, 2, D])
        xcT = sb("xcT", [P, 2, P])
        big = sb("big", [P, 2, HP, 2, P])
        kT = sb("kT", [P, HP, P])
        V = sb("V", [P, 2, HP * DK])
        e = sb("e", [P, 2, 512])
        pT = sb("pT", [P, 2, 512])
        oT = sb("oT", [P, HP, P])
        mx = sb("mx", [P, 2, 16])
        sm = sb("sm", [P, 2, 16])
        rc = sb("rc", [P, 2, 16])
        tmp = sb("tmp", [P, D])
        ss = sb("ss", [P, 4, 8])
        rn = sb("rn", [P, 4, 8])

        pj = [stack.enter_context(nc.psum_tensor(f"pj{i}", [P, 512], F32)) for i in range(2)]
        pt_ = stack.enter_context(nc.psum_tensor("turn", [P, 512], F32))
        sc = stack.enter_context(nc.psum_tensor("sc", [P, 1024], F32))
        pp = stack.enter_context(nc.psum_tensor("pp", [P, 512], F32))
        po = [stack.enter_context(nc.psum_tensor(f"po{i}", [P, 512], F32)) for i in range(2)]

        qz = big[:, 0]
        sq = big[:, 1].rearrange("p h a t -> p (h a t)")
        sqb = [sq[:, 0:512], sq[:, 512:1024]]
        t2b = [sq[:, 1024:1536], sq[:, 1536:2048]]
        bq = big[:, 0].rearrange("p h a t -> p (h a t)")
        qT = bq[:, 0:1024].rearrange("p (h t) -> p h t", h=HP)
        t1b = [bq[:, 1024:1536], bq[:, 1536:2048]]
        qn = sb("qn", [P, 2, 512])
        big2 = sb("big2", [P, 1024])

        xd = x.rearrange("b s d -> (b s) d").rearrange("(i p) d -> p i d", p=P)
        cd = ctx.rearrange("b s d -> (b s) d").rearrange("(i p) d -> p i d", p=P)
        od = out.rearrange("b s d -> (b s) d").rearrange("(i p) d -> p i d", p=P)

        def bc(ap, n):
            return ap.unsqueeze(len(ap.shape)).broadcast_to(list(ap.shape) + [n])

        def pbc(ap, n=P):
            return ap.partition_broadcast(n)

        s_ld = sem("loaded")
        loads = [0]
        layers = DEPTH if stop > 2 else 1

        ATT_LOADS = 4 * 16
        FFN_LOADS = (2 + 1 + 2 + 3 * 2 + 1) * 16

        wst1, wst3, wst2 = (w[:, :].rearrange("p (e d) -> p e d", e=NE) for w in (xq, xk, xv))
        sst = wqkv[:, 0:6 * P].rearrange("p (k e d) -> p k e d", k=3, e=2)
        eT = {1: mkn[:, :].rearrange("p (e d) -> p e d", e=NE), 3: mvn[:, :].rearrange("p (e d) -> p e d", e=NE),
              2: mkT[:, :, :]}
        sT = wqkv[:, 6 * P:12 * P].rearrange("p (k e d) -> p k e d", k=3, e=2)

        def expert_T(k, ex):
            return eT[k][:, ex, :] if ex < NE else sT[:, (1, 3, 2).index(k), ex - NE, :]

        def expert_natural(k, ex):
            return (dict(zip((1, 3, 2), (wst1, wst3, wst2)))[k][:, ex, :] if ex < NE
                    else sst[:, (1, 3, 2).index(k), ex - NE, :])

        TURNS = [(k, ex) for k in (1, 3, 2) for ex in range(NEX)]
        TURN4 = [TURNS[i:i + 4] for i in range(0, len(TURNS), 4)]

        block = stack.enter_context(nc.Block())

        def past_waits(eng, name):
            eng.sem_inc(sem(name), 1)

        def pipeline(eng, n, body, base=0):
            body((base, 0), None)
            with eng.Fori(1, n) as i:
                body((i + base, i), (i + (base - 1) if isinstance(base, int) else i + base - 1, i - 1))
            body(None, (base + (n - 1), n - 1))

        @block.sync
        def _(sp):
            def load(dst, src):
                sp.dma_start(dst, src, allow_slow_non_contiguous=True).then_inc(s_ld, 16)

            load(K[:, :], consts)
            load(X[:, :, :], xd)
            load(CT[:, :, :], cd)
            load(xq[:, :], wq_w)
            load(xk[:, :], wk_w)
            load(xv[:, :], wv_w)
            load(mkn[:, :], mk.rearrange("a m n -> (a m) n"))
            load(mvn[:, :], mv.rearrange("a m n -> (a m) n"))
            load(xo[:, :, :], wo_w.rearrange("(c p) n -> p c n", p=P))
            load(qb[:, :], wq_b.rearrange("(c p) -> p c", p=P))
            load(kb[:, :], wk_b.rearrange("(c p) -> p c", p=P))
            for par in range(2):
                load(vb[par * 64:par * 64 + 64, :, :],
                     pbc(wv_b.rearrange("(h a d) -> a h d", a=2, d=DK)[par], 64))
            load(ob[:, :], pbc(wo_b))
            load(gates[:, 0:1], pbc(g_xattn[0:1]))
            load(gates[:, 1:2], pbc(g_ffn[0:1]))
            load(gates[:, 2:3], pbc(g_xattn[1:2]))
            load(gates[:, 3:4], pbc(g_ffn[1:2]))
            load(lkv[:, :], w_kv)
            load(lq[:, :], w_q)
            load(lla[:, :], w_la)
            load(lpj[:, :], w_proj)
            load(lpb[:, :], pbc(b_proj))
            load(law[:, 0:1], pbc(att_weight))
            load(egw[:, :], gate_w)
            load(egb[:, :], pbc(gate_bias))

            if stop > 1:
                with sp.Fori(0, layers) as l:
                    sp.wait_ge(sem("d_wo"), l * NT)
                    sp.dma_start(wqkv[:, :], Wqkv[l, :, :]).then_inc(sem("att_loaded"), 16)
                    sp.dma_start(wo[:, :, :], Wo[l, :, :].rearrange("(c p) n -> p c n", p=P)).then_inc(sem("att_loaded"), 16)
                    sp.dma_start(qs[:, 0, :], pbc(q_scale[l, :])).then_inc(sem("att_loaded"), 16)
                    sp.dma_start(qs[:, 1, :], pbc(k_scale[l, :])).then_inc(sem("att_loaded"), 16)
                    sp.wait_ge(sem("f_res"), l * NF)

                    def fload(dst, src):
                        sp.dma_start(dst, src, allow_slow_non_contiguous=True).then_inc(sem("ffn_loaded"), 16)

                    fload(fw1[:, :], W1[l, :, :])
                    fload(fw2[:, 0:2, :], W2[l, 0:2 * P, :].rearrange("(c p) n -> p c n", p=P))
                    fload(fw2[0:FI - 2 * P, 2, :], W2[l, 2 * P:FI, :])
                    fload(fg[:, 0:1], ln_g[l, :].rearrange("(p a) -> p a", a=1))
                    fload(fg[:, 1:2], ln_b[l, :].rearrange("(p a) -> p a", a=1))
                    for k in range(2):
                        for j, (o, n) in enumerate(FBLK):
                            fload(fb1[0:n, k, j:j + 1], b1[l, k * FI + o:k * FI + o + n].rearrange("(p a) -> p a", a=1))
                    fload(fb2[:, :], b2[l, :].rearrange("(a n) -> a n", a=1))
            if stop > 3:
                sp.wait_ge(sem("d_wo"), layers * NT)
                for wst, src in ((wst1, w1), (wst3, w3), (wst2, w2)):
                    sp.dma_start(wst, src.rearrange("e i d -> i e d")).then_inc(sem("exp_loaded"), 16)
                for i, src in enumerate((sw1, sw3)):
                    sp.dma_start(sst[:, i, :, :], src.rearrange("(e i) d -> i e d", e=2)).then_inc(sem("exp_loaded"), 16)
                sp.dma_start(sst[:, 2, :, :], sw2.rearrange("d (e i) -> d e i", e=2)).then_inc(sem("exp_loaded"), 16)
                for m in range(NM):
                    sp.wait_ge(sem("m_out"), m + 1)
                    sp.dma_start(od[:, m * MT:m * MT + MT, :], X[:, m * MT:m * MT + MT, :]).then_inc(sem("stored"), 16)
                sp.wait_ge(sem("stored"), 16 * NM)
            else:
                if stop == 0:
                    sp.wait_ge(sem("n_y"), 1)
                elif stop == 1:
                    sp.wait_ge(sem("x_res"), NT)
                elif stop == 2:
                    sp.wait_ge(sem("f_res"), NF)
                elif stop == 3:
                    sp.wait_ge(sem("l_res"), NT)
                sp.dma_start(od, (Y if stop in (0, 2) else X)[:, :, :]).then_inc(sem("stored"), 16)
                sp.wait_ge(sem("stored"), 16)

        NLOAD = 26 * 16

        @block.gpsimd
        def _(pool):
            def rsqrt_many(n):
                pool.wait_ge(sem("n_var"), n)
                nc.gpsimd.tensor_scalar(var[:, :], var[:, :], EPS, None, ALU.add).then_inc(sem("n_eps"), 1)
                pool.wait_ge(sem("n_eps"), n)
                nc.gpsimd.tensor_tensor(rstd[:, :], var[:, :], nhalf, ALU.pow).then_inc(sem("n_rstd"), 1)

            def feed(pre, n_in, n_used):
                def f(g, t):
                    pool.wait_ge(sem(n_used), g)
                    nc.gpsimd.tensor_copy(xs[:, 0, :], Y[:, t, :])
                    nc.gpsimd.tensor_copy(xs[:, 1, :], CT[:, t, :]).then_inc(sem(n_in), 1)
                return f

            pool.wait_ge(s_ld, NLOAD)
            nc.gpsimd.memset(big[:, 0, :, :, :], 0.0).then_inc(sem("zeroed"), 1)
            rsqrt_many(1)
            if stop == 0:
                return
            pool.wait_ge(sem("n_y"), 1)
            copy_in = feed("x", "x_in", "x_T")

            def x_body(a, b):
                if a:
                    copy_in(*a)
                if b:
                    g, _ = b
                    for k in range(HP):
                        pool.wait_ge(sem("x_rc"), g * 8 + (k + 1))
                        pool.wait_ge(sem("x_e"), g * 8 + (k + 1))
                        ev = e[:, k % 2, 0:384].rearrange("p (a t) -> p a t", a=2)
                        nc.gpsimd.tensor_tensor(ev, ev, bc(rc[:, k % 2, 0:2], 192), ALU.mult).then_inc(sem("x_p"), 1)

            pipeline(pool, NT, x_body)
            if stop == 1:
                return
            rsqrt_many(2)
            pool.wait_ge(sem("n_y"), 2)
            nc.gpsimd.memset(xcT[:, 0, :], 0.0).then_inc(sem("zeroed"), 1)

            def d_body(a, b):
                if a:
                    g, t = a
                    pool.wait_ge(sem("y_ready"), g + 1)
                    pool.wait_ge(sem("d_xT"), g)
                    past_waits(pool, "pool_went_on")
                    nc.gpsimd.tensor_copy(xs[:, 0, :], Y[:, t, :]).then_inc(sem("d_xin"), 1)

                def rope_sum(c):
                    if a:
                        g, _ = a
                        pool.wait_ge(sem("d_rope"), g * 4 + (c + 1))
                        nc.gpsimd.tensor_tensor(t1b[c % 2], t1b[c % 2], t2b[c % 2], ALU.add).then_inc(sem("d_u"), 1)
                        pool.wait_ge(sem("d_ss"), g * 4 + (c + 1))
                        past_waits(pool, "pool_went_on")
                        nc.gpsimd.tensor_scalar(ss[:, c, :], ss[:, c, :], 1e-24, None, ALU.max).then_inc(sem("d_clamp"), 1)
                        pool.wait_ge(sem("d_clamp"), g * 4 + (c + 1))
                        nc.gpsimd.tensor_tensor(rn[:, c, :], ss[:, c, :], nhalf[:, 0:8], ALU.pow).then_inc(sem("d_r"), 1)

                def probs(h):
                    if b:
                        g, _ = b
                        pool.wait_ge(sem("d_rc"), g * 2 + (h + 1))
                        pool.wait_ge(sem("d_e"), g * 2 + (h + 1))
                        ev = e[:, h, :].rearrange("p (a t) -> p a t", t=S)
                        nc.gpsimd.tensor_tensor(ev, ev, bc(rc[:, h, 0:8], S), ALU.mult).then_inc(sem("d_p"), 1)

                rope_sum(0)
                rope_sum(1)
                probs(0)
                probs(1)
                rope_sum(2)
                rope_sum(3)

            def f_body(a, b):
                if a:
                    g, t = a
                    pool.wait_ge(sem("d_res"), g * FT + FT)
                    pool.wait_ge(sem("f_xn"), g)
                    past_waits(pool, "pool_went_on")
                    nc.gpsimd.tensor_copy(xs[:, :, :], Y[:, bass.ds(t * FT, FT), :]).then_inc(sem("f_in"), 1)
                    pool.wait_ge(sem("f_mv"), g + 1)
                    nc.gpsimd.tensor_tensor(m2[:, 0:FT], var[:, 0:FT], const("eps")[:, 0:FT], ALU.add).then_inc(sem("f_eps"), 1)
                    pool.wait_ge(sem("f_eps"), g + 1)
                    nc.gpsimd.tensor_tensor(rstd[:, 0:FT], m2[:, 0:FT], nhalf[:, 0:FT], ALU.pow).then_inc(sem("f_rstd"), 1)

            with pool.Fori(0, layers) as l:
                pool.wait_ge(sem("f_xn"), l * NF)
                pipeline(pool, NT, d_body, l * NT)
                pool.wait_ge(sem("d_xT"), l * NT + NT)
                pipeline(pool, NF, f_body, l * NF)
            if stop == 2:
                return
            rsqrt_many(3)
            pool.wait_ge(sem("n_y"), 3)
            lcopy = feed("l", "l_in", "l_T")
            km = big[:, :, :, :, :].rearrange("p w h a t -> p w (h a) t")

            def l_body(a, b):
                if a:
                    g, t = a
                    lcopy(g, t)
                    pool.wait_ge(sem("l_kT"), g + 1)
                    pool.wait_ge(sem("l_s"), g)
                    kk = kT[:, 0, :].rearrange("p (b t) -> p b t", b=BT)
                    for bb in range(BT):
                        last = nc.gpsimd.tensor_tensor(
                            km[:, bb, :, 0:S], kk[:, bb, :].unsqueeze(1).broadcast_to([P, L1H, S]),
                            bc(const("headmask"), S), ALU.mult)
                    last.then_inc(sem("l_km"), 1)
                if b:
                    g, _ = b
                    pool.wait_ge(sem("l_c1"), g + 1)
                    pool.wait_ge(sem("l_z"), g + 1)
                    e1 = e[:, :, :].rearrange("p a (h t) -> p (a h) t", t=S)
                    nc.gpsimd.tensor_tensor(e1, e1, bc(sm[:, 1, :], S), ALU.mult).then_inc(sem("l_m1"), 1)
                    pool.wait_ge(sem("l_m2"), g + 1)
                    pool.wait_ge(sem("l_m1"), g + 1)
                    nc.gpsimd.tensor_tensor(e[:, :, :].rearrange("p a c -> p (a c)"), e[:, :, :].rearrange("p a c -> p (a c)"), big2[:, :], ALU.add).then_inc(sem("l_p"), 1)

            pipeline(pool, NT, l_body)
            if stop == 3:
                return
            rsqrt_many(4)
            pool.wait_ge(sem("n_y"), 4)

            def r_body(a, b):
                if a:
                    g, t = a
                    pool.wait_ge(sem("r_T"), g)
                    nc.gpsimd.tensor_copy(xs[:, 0, :], Y[:, t, :]).then_inc(sem("r_in"), 1)

            pipeline(pool, NT, r_body)

        @block.scalar
        def _(act):
            act.wait_ge(s_ld, NLOAD)
            nc.scalar.activation(tg[:, :], gates[:, :], ACT.Tanh).then_inc(sem("tanh"), 1)
            nc.scalar.copy(identb[:, :], ident)
            for i in range(4 * BT):
                last = nc.scalar.copy(bandb[:, i // BT, i % BT, :], const("band"))
            last.then_inc(sem("cast"), 1)
            for i in range(2):
                act.wait_ge(sem("mk_T"), i + 1)
                nc.scalar.copy(mkT[:, 4 * i:4 * i + 4, :].rearrange("p h m -> p (h m)"), pt_[:, :]).then_inc(sem("mk_c"), 1)
            if stop == 0:
                return

            def x_body(a, b):
                if a:
                    g, _ = a
                    act.wait_ge(sem("x_T"), g + 1)
                    act.wait_ge(sem("x_proj"), g * 6)
                    nc.scalar.copy(xcT[:, :, :].rearrange("p a t -> p (a t)"), pt_[:, 0:2 * P]).then_inc(sem("x_xcT"), 1)
                if b:
                    g, _ = b
                    for k in range(HP + 2):
                        if k < HP:
                            act.wait_ge(sem("x_sub"), g * 8 + (k + 1))
                            nc.scalar.activation(e[:, k % 2, 0:384], e[:, k % 2, 0:384], ACT.Exp, scale=DK ** -0.5).then_inc(sem("x_e"), 1)
                        j = k - 1
                        if 0 <= j < HP:
                            act.wait_ge(sem("x_pt"), g * 8 + (j + 1))
                            act.wait_ge(sem("x_pv"), g * 8 + (j - 1 if j >= 2 else 0))
                            nc.scalar.copy(pT[:, j % 2, 0:384], pp[:, 0:384]).then_inc(sem("x_ptc"), 1)
                        j = k - 2
                        if j in (3, 7):
                            act.wait_ge(sem("x_pv"), g * 8 + (j + 1))
                            act.wait_ge(sem("x_wo"), g)
                            nc.scalar.copy(oT[:, j - 3:j + 1, :].rearrange("p h t -> p (h t)"), po[0][:, :]).then_inc(sem("x_o"), 1)

            pipeline(act, NT, x_body)
            if stop == 1:
                return
            act.wait_ge(sem("zeroed"), 2)

            def d_body(a, b):
                def square(c):
                    if a:
                        g, _ = a
                        act.wait_ge(sem("d_proj"), g * 6 + (c + 1))
                        act.wait_ge(sem("d_ss"), g * 4 + (c - 1 if c >= 2 else 0))
                        nc.scalar.activation(sqb[c % 2], pj[c % 2][:, :], ACT.Square).then_inc(sem("d_sq"), 1)

                def turned(c):
                    if a:
                        g, _ = a
                        act.wait_ge(sem("d_TT"), g * 4 + (c + 1))
                        act.wait_ge(sem("d_s"), g * 2)
                        dst = (qT if c < 2 else kT)[:, (c % 2) * 4:(c % 2) * 4 + 4, :]
                        nc.scalar.copy(dst.rearrange("p h t -> p (h t)"), pt_[:, :]).then_inc(sem("d_qkT"), 1)

                def values(c):
                    if a:
                        g, _ = a
                        act.wait_ge(sem("d_proj"), g * 6 + (c + 5))
                        act.wait_ge(sem("d_pv"), g * 2)
                        nc.scalar.copy(V[:, c, :], pj[c][:, :]).then_inc(sem("d_v"), 1)

                def exps(h):
                    if b:
                        g, _ = b
                        act.wait_ge(sem("d_sub"), g * 2 + (h + 1))
                        nc.scalar.activation(e[:, h, :], e[:, h, :], ACT.Exp, scale=QK_SCALE).then_inc(sem("d_e"), 1)

                def probsT(h):
                    if b:
                        g, _ = b
                        act.wait_ge(sem("d_pt"), g * 2 + (h + 1))
                        act.wait_ge(sem("d_pv"), g * 2)
                        nc.scalar.copy(pT[:, h, :], pp[:, :]).then_inc(sem("d_ptc"), 1)

                def outT(h):
                    if b:
                        g, _ = b
                        act.wait_ge(sem("d_pv"), g * 2 + (h + 1))
                        act.wait_ge(sem("d_wo"), g)
                        ov = oT[:, 4 * h:4 * h + 4, :].rearrange("p h (b s) -> p h b s", b=BT)
                        for bb in range(BT):
                            last = nc.scalar.copy(ov[:, :, bb, :], po[bb][:, 0:256].rearrange("p (h s) -> p h s", h=4))
                        last.then_inc(sem("d_o"), 1)

                if a:
                    g, _ = a
                    act.wait_ge(sem("d_xT"), g + 1)
                    act.wait_ge(sem("d_proj"), g * 6)
                    nc.scalar.copy(xcT[0:64, 0, :], pt_[0:64, 0:P])
                    xv_ = xcT[64:P, 0, :].rearrange("p (b s) -> p b s", b=BT)
                    tv_ = pt_[64:P, 0:P].rearrange("p (b s) -> p b s", b=BT)
                    nc.scalar.copy(xv_[:, :, 1:S], tv_[:, :, 0:S - 1]).then_inc(sem("d_xsT"), 1)
                square(0)
                exps(0)
                square(1)
                exps(1)
                turned(0)
                probsT(0)
                square(2)
                turned(1)
                outT(0)
                square(3)
                probsT(1)
                turned(2)
                outT(1)
                values(0)
                turned(3)
                values(1)

            def f_body(a, b):
                if b:
                    g, _ = b
                    for j, (_, n) in enumerate(FBLK):
                        act.wait_ge(sem("f_h"), g * 3 + (j + 1))
                        act.wait_ge(sem("f_hT"), g * 3 + (j - 1 if j >= 2 else 0))
                        nc.scalar.activation(e[0:n, j % 2, 0:256], pj[j % 2][0:n, 0:256], ACT.Gelu, bias=fb1[0:n, 1, j:j + 1]).then_inc(sem("f_gl"), 1)
                if a:
                    g, _ = a
                    act.wait_ge(sem("f_xnT"), g + 1)
                    act.wait_ge(sem("f_h"), g * 3)
                    nc.scalar.activation(kT[:, 0:2, :].rearrange("p a t -> p (a t)"), pt_[:, 0:2 * P], ACT.Identity, scale=fg[:, 0:1], bias=fg[:, 1:2]).then_inc(sem("f_xT"), 1)

            with act.Fori(0, layers) as l:
                act.wait_ge(sem("f_h"), l * (3 * NF))
                pipeline(act, NT, d_body, l * NT)
                act.wait_ge(sem("d_s"), l * (2 * NT) + 2 * NT)
                act.wait_ge(sem("d_pt"), l * (2 * NT) + 2 * NT)
                act.wait_ge(sem("ffn_loaded"), l * FFN_LOADS + FFN_LOADS)
                pipeline(act, NF, f_body, l * NF)
            if stop == 2:
                return

            def l_body(a, b):
                if a:
                    g, _ = a
                    act.wait_ge(sem("l_T"), g + 1)
                    act.wait_ge(sem("l_proj"), g)
                    nc.scalar.copy(xcT[:, :, :].rearrange("p a t -> p (a t)"), pt_[:, 0:2 * P]).then_inc(sem("l_xcT"), 1)
                if b:
                    g, _ = b
                    ef = e[:, :, :].rearrange("p a c -> p (a c)")
                    act.wait_ge(sem("l_sub"), g + 1)
                    nc.scalar.activation(ef, ef, ACT.Exp, scale=L1D ** -0.5).then_inc(sem("l_e"), 1)
                    act.wait_ge(sem("l_sub2"), g + 1)
                    nc.scalar.activation(big2[:, :], big2[:, :], ACT.Exp).then_inc(sem("l_e2"), 1)
                    for h in range(2):
                        act.wait_ge(sem("l_pt"), g * 2 + (h + 1))
                        nc.scalar.copy(pT[:, h, :], pp[:, :]).then_inc(sem("l_ptc"), 1)
                    act.wait_ge(sem("l_pv"), g + 1)
                    ov = tmp[:, :].rearrange("p (h a d) -> p h a d", a=2, d=L1D)
                    for par in range(2):
                        last = nc.scalar.copy(ov[:, :, par, :], po[par][:, 0:64].rearrange("p (h d) -> p h d", d=L1D))
                    last.then_inc(sem("l_o"), 1)
                    act.wait_ge(sem("l_oT"), g + 1)
                    nc.scalar.copy(oT[:, 0, :], po[0][:, 128:256]).then_inc(sem("l_oTc"), 1)

            pipeline(act, NT, l_body)
            if stop == 3:
                return
            for i, some in enumerate(TURN4):
                act.wait_ge(sem("w_T"), i + 1)
                for j, (k, ex) in enumerate(some):
                    last = nc.scalar.copy(expert_T(k, ex), pt_[:, j * P:j * P + P])
                last.then_inc(sem("w_c"), 1)
            act.wait_ge(sem("g_T"), 1)
            nc.scalar.copy(egT[:, :], pp[:, 0:NE]).then_inc(sem("g_c"), 1)

            def r_body(a, b):
                if a:
                    g, t = a
                    act.wait_ge(sem("r_T"), g + 1)
                    act.wait_ge(sem("r_lg"), g)
                    nc.scalar.copy(xcT[:, 0, :], pt_[:, 0:P]).then_inc(sem("r_xT"), 1)
                    act.wait_ge(sem("r_xT"), g + 1)
                    nc.scalar.copy(CT[:, t, :], xcT[:, 0, :]).then_inc(sem("r_XT"), 1)
                if b:
                    g, _ = b
                    act.wait_ge(sem("r_mx"), g + 1)
                    nc.scalar.activation(ss[:, 0, :], ss[:, 1, :], ACT.Exp, bias=mx[:, 0, 0:1], accum_out=sm[:, 0, 0:1]).then_inc(sem("r_e"), 1)

            pipeline(act, NT, r_body)

            for m in range(1):
                with act.Fori(0, NM) as m:
                    for ex in range(NEX):
                        act.wait_ge(sem("m_h"), m * NEX + (ex + 1))
                        act.wait_ge(sem("m_hT"), m * NEX + ex)
                        nc.scalar.activation(e[:, 0, :], pj[0][:, :], ACT.Silu).then_inc(sem("m_silu"), 1)

        @block.vector
        def _(dve):
            def normalise(n, combine):
                with dve.Fori(0, NT) as t:
                    if combine:
                        nc.vector.scalar_tensor_tensor(X[:, t, :], Y[:, t, :], tg[:, 1:2], X[:, t, :], ALU.mult, ALU.add).then_inc(sem("n_x"), 1)
                        dve.wait_ge(sem("n_x"), t + 1)
                    nc.vector.bn_stats(st[:, t, :], X[:, t, :]).then_inc(sem("n_st"), 1)
                dve.wait_ge(sem("n_st"), n * NT)
                nc.vector.tensor_tensor(mean[:, :], st[:, :, 1], st[:, :, 4], ALU.add)
                nc.vector.tensor_tensor(dif[:, :], st[:, :, 1], st[:, :, 4], ALU.subtract)
                nc.vector.tensor_tensor(m2[:, :], st[:, :, 2], st[:, :, 5], ALU.add).then_inc(sem("n_1"), 1)
                dve.wait_ge(sem("n_1"), n)
                nc.vector.tensor_scalar(mean[:, :], mean[:, :], 0.5, None, ALU.mult)
                nc.vector.scalar_tensor_tensor(dif[:, :], dif[:, :], 0.25, dif[:, :], ALU.mult, ALU.mult).then_inc(sem("n_2"), 1)
                dve.wait_ge(sem("n_2"), n)
                nc.vector.scalar_tensor_tensor(var[:, :], m2[:, :], 1.0 / D, dif[:, :], ALU.mult, ALU.add).then_inc(sem("n_var"), 1)
                dve.wait_ge(sem("n_rstd"), n)
                with dve.Fori(0, NT) as t:
                    nc.vector.tensor_scalar(Y[:, t, :], X[:, t, :], mean[:, bass.ds(t, 1)], rstd[:, bass.ds(t, 1)], ALU.subtract, ALU.mult).then_inc(sem("y_ready" if n == 2 else "n_t"), 1)
                dve.wait_ge(sem("y_ready" if n == 2 else "n_t"), NT * (n if n == 1 else 1 if n == 2 else n - 1))
                nc.vector.tensor_copy(tmp[:, 0:1], mean[:, 0:1]).then_inc(sem("n_y"), 1)

            dve.wait_ge(s_ld, NLOAD)
            nc.vector.tensor_scalar(law[:, 1:2], law[:, 0:1], -1.0, 1.0, ALU.mult, ALU.add)
            dve.wait_ge(sem("tanh"), 1)
            normalise(1, False)
            if stop == 0:
                return
            dve.wait_ge(sem("zeroed"), 1)

            def x_body(a, b):
                def leave(c):
                    g, _ = a
                    dve.wait_ge(sem("x_proj"), g * 6 + (c + 1))
                    pv4 = pj[c % 2][:, :].rearrange("p (h t) -> p h t", h=4)
                    if c < 2:
                        hs = slice(4 * c, 4 * c + 4)
                        for par in range(2):
                            r = slice(par * 64, par * 64 + 64)
                            last = nc.vector.tensor_tensor(qz[r, hs, par, :], pv4[r], bc(qb[r, hs], P), ALU.add)
                    elif c < 4:
                        hs = slice(4 * (c - 2), 4 * (c - 2) + 4)
                        last = nc.vector.tensor_tensor(kT[:, hs, :], pv4, bc(kb[:, hs], P), ALU.add)
                    else:
                        dve.wait_ge(sem("x_pv"), g * 8)
                        last = nc.vector.tensor_tensor(V[:, c - 4, :], pj[c % 2][:, :], vb[:, :, :].rearrange("p h d -> p (h d)"), ALU.add)
                    last.then_inc(sem("x_ev"), 1)

                def smax(k):
                    g, _ = b
                    dve.wait_ge(sem("x_s"), g * 8 + (k + 1))
                    sv = sc[:, (k % 2) * 512:(k % 2) * 512 + 384].rearrange("p (a t) -> p a t", a=2)
                    nc.vector.tensor_reduce(mx[:, k % 2, 0:2], sv, AX, ALU.max).then_inc(sem("x_mx"), 1)
                    dve.wait_ge(sem("x_mx"), g * 8 + (k + 1))
                    dve.wait_ge(sem("x_pt"), g * 8 + (k - 1 if k >= 2 else 0))
                    ev = e[:, k % 2, 0:384].rearrange("p (a t) -> p a t", a=2)
                    nc.vector.tensor_tensor(ev, sv, bc(mx[:, k % 2, 0:2], 192), ALU.subtract).then_inc(sem("x_sub"), 1)

                def sums(k):
                    g, _ = b
                    dve.wait_ge(sem("x_e"), g * 8 + (k + 1))
                    ev = e[:, k % 2, 0:384].rearrange("p (a t) -> p a t", a=2)
                    nc.vector.tensor_reduce(sm[:, k % 2, 0:2], ev, AX, ALU.add).then_inc(sem("x_sum"), 1)
                    dve.wait_ge(sem("x_sum"), g * 8 + (k + 1))
                    nc.vector.reciprocal(rc[:, k % 2, 0:2], sm[:, k % 2, 0:2]).then_inc(sem("x_rc"), 1)

                if b:
                    for k in range(HP + 1):
                        if k < HP:
                            smax(k)
                        if k > 0:
                            sums(k - 1)
                if a:
                    for c in range(6):
                        leave(c)
                if b:
                    g, t = b
                    dve.wait_ge(sem("x_wo"), g + 1)
                    nc.vector.tensor_tensor(tmp[:, :], po[1][:, 0:D], ob[:, :], ALU.add).then_inc(sem("x_tmp"), 1)
                    dve.wait_ge(sem("x_tmp"), g + 1)
                    nc.vector.scalar_tensor_tensor(X[:, t, :], tmp[:, :], tg[:, 0:1], X[:, t, :], ALU.mult, ALU.add).then_inc(sem("x_res"), 1)

            pipeline(dve, NT, x_body)
            if stop == 1:
                return
            dve.wait_ge(sem("x_res"), NT)
            normalise(2, False)

            def d_body(a, b):
                def rope(c):
                    if a:
                        g, _ = a
                        w = c // 2
                        dve.wait_ge(sem("d_sq"), g * 4 + (c + 1))
                        dve.wait_ge(sem("d_u"), g * 4 + (c - 1 if c >= 2 else 0))
                        pv = pj[c % 2][:, :].rearrange("p (h d) -> p h d", d=DK)
                        t1v = t1b[c % 2].rearrange("p (h d) -> p h d", d=DK)
                        t2v = t2b[c % 2].rearrange("p (h d) -> p h d", d=DK)

                        def table(tb, lo, hi):
                            return tb[:, w, lo:hi].unsqueeze(1).broadcast_to([P, 8, hi - lo])

                        nc.vector.tensor_tensor(t1v, pv, table(rc_, 0, DK), ALU.mult)
                        nc.vector.tensor_tensor(t2v[:, :, 0:32], pv[:, :, 32:64], table(rs_, 0, 32), ALU.mult)
                        nc.vector.tensor_tensor(t2v[:, :, 32:64], pv[:, :, 0:32], table(rs_, 32, 64), ALU.mult).then_inc(sem("d_rope"), 1)
                        dve.wait_ge(sem("d_r"), g * 4)
                        nc.vector.tensor_reduce(ss[:, c, :], sqb[c % 2].rearrange("p (h d) -> p h d", d=DK), AX, ALU.add).then_inc(sem("d_ss"), 1)

                def unit(c):
                    if a:
                        g, _ = a
                        dve.wait_ge(sem("d_r"), g * 4 + (c + 1))
                        dve.wait_ge(sem("d_u"), g * 4 + (c + 1))
                        dve.wait_ge(sem("d_TT"), g * 4 + (c - 1 if c >= 2 else 0))
                        nc.vector.tensor_tensor(qn[:, c % 2, :].rearrange("p (h d) -> p h d", d=DK),
                                                t1b[c % 2].rearrange("p (h d) -> p h d", d=DK), bc(rn[:, c, :], DK), ALU.mult).then_inc(sem("d_qn"), 1)

                def smax(h):
                    if b:
                        g, _ = b
                        dve.wait_ge(sem("d_s"), g * 2 + (h + 1))
                        sv = sc[:, h * 512:h * 512 + 512].rearrange("p (a t) -> p a t", t=S)
                        nc.vector.tensor_reduce(mx[:, h, 0:8], sv, AX, ALU.max).then_inc(sem("d_mx"), 1)
                        dve.wait_ge(sem("d_mx"), g * 2 + (h + 1))
                        dve.wait_ge(sem("d_pt"), g * 2)
                        nc.vector.tensor_tensor(e[:, h, :].rearrange("p (a t) -> p a t", t=S), sv, bc(mx[:, h, 0:8], S), ALU.subtract).then_inc(sem("d_sub"), 1)

                def sums(h):
                    if b:
                        g, _ = b
                        dve.wait_ge(sem("d_e"), g * 2 + (h + 1))
                        dve.wait_ge(sem("d_p"), g * 2)
                        nc.vector.tensor_reduce(sm[:, h, 0:8], e[:, h, :].rearrange("p (a t) -> p a t", t=S), AX, ALU.add).then_inc(sem("d_sum"), 1)
                        dve.wait_ge(sem("d_sum"), g * 2 + (h + 1))
                        nc.vector.reciprocal(rc[:, h, 0:8], sm[:, h, 0:8]).then_inc(sem("d_rc"), 1)

                smax(0)
                rope(0)
                smax(1)
                rope(1)
                sums(0)
                unit(0)
                sums(1)
                rope(2)
                unit(1)
                rope(3)
                unit(2)
                unit(3)
                if b:
                    g, t = b
                    dve.wait_ge(sem("d_wo"), g + 1)
                    nc.vector.tensor_tensor(Y[:, t, :], po[0][:, 256:256 + D], Y[:, t, :], ALU.add).then_inc(sem("d_res"), 1)

            def f_body(a, b):
                if b:
                    g, _ = b
                    for j, (_, n) in enumerate(FBLK):
                        dve.wait_ge(sem("f_gl"), g * 3 + (j + 1))
                        dve.wait_ge(sem("f_y"), g)
                        nc.vector.scalar_tensor_tensor(big2[0:n, 256 * j:256 * j + 256], pj[j % 2][0:n, 256:512], fb1[0:n, 0, j:j + 1], e[0:n, j % 2, 0:256], ALU.add, ALU.mult).then_inc(sem("f_hT"), 1)
                if a:
                    g, _ = a
                    dve.wait_ge(sem("f_sh"), g + 1)
                    dve.wait_ge(sem("f_in"), g + 1)
                    for i in range(FT):
                        nc.vector.bn_stats(st[:, 2 * i, :], xs[:, i, 0:64])
                        last = nc.vector.bn_stats(st[:, 2 * i + 1, :], pt_[:, 64 * i:64 * i + 64])
                    last.then_inc(sem("f_st"), 1)
                    dve.wait_ge(sem("f_st"), g + 1)
                    dve.wait_ge(sem("f_rstd"), g)
                    nc.vector.tensor_copy(tmp[:, 0:1], fg[:, 0:1])
                    for i in range(FT):
                        last = nc.vector.bn_aggr(dif[:, 2 * i:2 * i + 2], st[:, 2 * i:2 * i + 2, :].rearrange("p a c -> p (a c)"))
                    last.then_inc(sem("f_ag"), 1)
                    dve.wait_ge(sem("f_ag"), g + 1)
                    nc.vector.tensor_copy(var[:, 0:FT], dif[:, 1:2 * FT:2]).then_inc(sem("f_mv"), 1)
                    dve.wait_ge(sem("f_rstd"), g + 1)
                    dve.wait_ge(sem("f_xnT"), g)
                    for i in range(FT):
                        nc.vector.tensor_scalar(qn[:, 0, 128 * i:128 * i + 64], xs[:, i, 0:64], dif[:, 2 * i:2 * i + 1], rstd[:, i:i + 1], ALU.subtract, ALU.mult)
                        last = nc.vector.tensor_scalar(qn[:, 0, 128 * i + 64:128 * i + 128], pt_[:, 64 * i:64 * i + 64], dif[:, 2 * i:2 * i + 1], rstd[:, i:i + 1], ALU.subtract, ALU.mult)
                    last.then_inc(sem("f_xn"), 1)
                if b:
                    g, t = b
                    dve.wait_ge(sem("f_y"), g + 1)
                    nc.vector.tensor_tensor(Y[:, bass.ds(t * FT, FT), :], sc[:, 0:2 * D].rearrange("p (a d) -> p a d", a=2), Y[:, bass.ds(t * FT, FT), :], ALU.add).then_inc(sem("y_ready"), FT)
                    nc.vector.tensor_copy(tmp[:, 1:2], fg[:, 1:2]).then_inc(sem("f_res"), 1)

            with dve.Fori(0, layers) as l:
                dve.wait_ge(sem("att_loaded"), l * ATT_LOADS + ATT_LOADS)
                dve.wait_ge(sem("d_rope"), l * (NT * 4))
                for w, (cn, sn) in enumerate((("qcos", "qsin"), ("kcos", "ksin"))):
                    nc.vector.tensor_tensor(rc_[:, w, :], const(cn), qs[:, w, :], ALU.mult)
                    nc.vector.tensor_tensor(rs_[:, w, 0:32], const(sn)[:, 0:32], qs[:, w, 32:64], ALU.mult)
                    last = nc.vector.tensor_tensor(rs_[:, w, 32:64], const(sn)[:, 32:64], qs[:, w, 0:32], ALU.mult)
                last.then_inc(sem("tables"), 1)
                dve.wait_ge(sem("tables"), l + 1)
                dve.wait_ge(sem("f_xnT"), l * NF)
                pipeline(dve, NT, d_body, l * NT)
                dve.wait_ge(sem("d_TT"), l * (4 * NT) + 4 * NT)
                dve.wait_ge(sem("ffn_loaded"), l * FFN_LOADS + FFN_LOADS)
                pipeline(dve, NF, f_body, l * NF)
            if stop == 2:
                return
            dve.wait_ge(sem("f_res"), layers * NF)
            dve.wait_ge(sem("y_ready"), NT * (layers + 1))
            normalise(3, True)
            gm = ss[0:L1H, 0, :]
            gb = qn[0:L1H, 0, 0:P]

            def l_body(a, b):
                if b:
                    g, _ = b
                    scv = sc[:, :].rearrange("p (h t) -> p h t", t=S)
                    e1 = e[:, :, :].rearrange("p a (h t) -> p (a h) t", t=S)
                    e2 = big2[:, :].rearrange("p (h t) -> p h t", t=S)
                    dve.wait_ge(sem("l_s"), g + 1)
                    nc.vector.tensor_reduce(mx[:, 0, :], scv, AX, ALU.max).then_inc(sem("l_mx"), 1)
                    dve.wait_ge(sem("l_mx"), g + 1)
                    dve.wait_ge(sem("l_pt"), g * 2)
                    nc.vector.tensor_tensor(e1, scv, bc(mx[:, 0, :], S), ALU.subtract).then_inc(sem("l_sub"), 1)
                    dve.wait_ge(sem("l_e"), g + 1)
                    nc.vector.tensor_reduce(sm[:, 0, :], e1, AX, ALU.add).then_inc(sem("l_sum"), 1)
                    dve.wait_ge(sem("l_sum"), g + 1)
                    nc.vector.reciprocal(rc[:, 0, :], sm[:, 0, :]).then_inc(sem("l_rc"), 1)
                    dve.wait_ge(sem("l_rc"), g + 1)
                    nc.vector.tensor_tensor(rc[:, 1, :], pt_[:, 2 * P:2 * P + L1H], rc[:, 0, :], ALU.mult)
                    nc.vector.tensor_scalar(sm[:, 1, :], rc[:, 0, :], law[:, 1:2], None, ALU.mult).then_inc(sem("l_c1"), 1)
                    dve.wait_ge(sem("l_c1"), g + 1)
                    nc.vector.tensor_tensor(e2, e1, bc(rc[:, 1, :], S), ALU.mult).then_inc(sem("l_z"), 1)
                    dve.wait_ge(sem("l_z"), g + 1)
                    nc.vector.tensor_reduce(mx[:, 1, :], e2, AX, ALU.max).then_inc(sem("l_mx2"), 1)
                    dve.wait_ge(sem("l_mx2"), g + 1)
                    nc.vector.tensor_tensor(e2, e2, bc(mx[:, 1, :], S), ALU.subtract).then_inc(sem("l_sub2"), 1)
                    dve.wait_ge(sem("l_e2"), g + 1)
                    nc.vector.tensor_reduce(sm[:, 0, :], e2, AX, ALU.add).then_inc(sem("l_sum2"), 1)
                    dve.wait_ge(sem("l_sum2"), g + 1)
                    nc.vector.reciprocal(rc[:, 0, :], sm[:, 0, :]).then_inc(sem("l_rc2"), 1)
                    dve.wait_ge(sem("l_rc2"), g + 1)
                    nc.vector.tensor_scalar(rc[:, 0, :], rc[:, 0, :], law[:, 0:1], None, ALU.mult).then_inc(sem("l_w2"), 1)
                    dve.wait_ge(sem("l_w2"), g + 1)
                    nc.vector.tensor_tensor(e2, e2, bc(rc[:, 0, :], S), ALU.mult).then_inc(sem("l_m2"), 1)
                if a:
                    g, _ = a
                    dve.wait_ge(sem("l_proj"), g + 1)
                    dve.wait_ge(sem("l_km"), g)
                    nc.vector.tensor_copy(kT[:, 0, :], pj[0][:, P:2 * P]).then_inc(sem("l_kT"), 1)
                    nc.vector.tensor_copy(kT[:, 1, :], pj[0][:, 0:P])
                    gv = pj[0][0:L1H, 2 * P:3 * P].rearrange("p (b t) -> p b t", b=BT)
                    nc.vector.tensor_reduce(gm[:, 0:2], gv, AX, ALU.max)
                    nc.vector.tensor_reduce(gm[:, 2:4], gv, AX, ALU.add).then_inc(sem("l_gm"), 1)
                    dve.wait_ge(sem("l_gm"), g + 1)
                    nc.vector.tensor_scalar(gm[:, 2:4], gm[:, 2:4], 0.5 / S, None, ALU.mult).then_inc(sem("l_g1"), 1)
                    dve.wait_ge(sem("l_g1"), g + 1)
                    nc.vector.scalar_tensor_tensor(gm[:, 4:6], gm[:, 0:2], 0.5, gm[:, 2:4], ALU.mult, ALU.add).then_inc(sem("l_g2"), 1)
                    dve.wait_ge(sem("l_g2"), g + 1)
                    dve.wait_ge(sem("l_gr"), g)
                    nc.vector.tensor_copy(gb.rearrange("p (b s) -> p b s", b=BT), bc(gm[:, 4:6], S)).then_inc(sem("l_gb"), 1)
                    dve.wait_ge(sem("l_pv"), g)
                    nc.vector.tensor_copy(V[:, 0, 0:P], pj[0][:, 3 * P:4 * P]).then_inc(sem("l_V"), 1)
                if b:
                    g, t = b
                    dve.wait_ge(sem("l_pr"), g + 1)
                    nc.vector.tensor_tensor(oT[:, 1, :], po[1][:, P:2 * P], lpb[:, :], ALU.add).then_inc(sem("l_tmp"), 1)
                    dve.wait_ge(sem("l_tmp"), g + 1)
                    nc.vector.scalar_tensor_tensor(X[:, t, :], oT[:, 1, :], tg[:, 2:3], X[:, t, :], ALU.mult, ALU.add).then_inc(sem("l_res"), 1)

            pipeline(dve, NT, l_body)
            if stop == 3:
                return
            dve.wait_ge(sem("l_res"), NT)
            normalise(4, False)

            idx = sb("idx", [P, 8], U32)
            idf = sb("idf", [P, 8])

            def r_body(a, b):
                if b:
                    g, t = b
                    lg = pp[:, 0:NE]
                    dve.wait_ge(sem("r_lg"), g + 1)
                    nc.vector.tensor_copy(ss[:, 1, :], lg)
                    nc.vector.tensor_reduce(mx[:, 0, 0:1], lg, AX, ALU.max, negate=True).then_inc(sem("r_mx"), 1)
                    dve.wait_ge(sem("r_e"), g + 1)
                    nc.vector.reciprocal(rc[:, 0, 0:1], sm[:, 0, 0:1]).then_inc(sem("r_rc"), 1)
                    dve.wait_ge(sem("r_rc"), g + 1)
                    nc.vector.tensor_scalar(ss[:, 2, :], ss[:, 0, :], rc[:, 0, 0:1], None, ALU.mult)
                    nc.vector.scalar_tensor_tensor(ss[:, 3, :], ss[:, 0, :], rc[:, 0, 0:1], egb[:, :], ALU.mult, ALU.add).then_inc(sem("r_sb"), 1)
                    dve.wait_ge(sem("r_sb"), g + 1)
                    nc.vector.tensor_copy(tmp[:, 0:1], law[:, 0:1])
                    nc.vector.max(rn[:, 0, :], ss[:, 3, :]).then_inc(sem("r_top"), 1)
                    dve.wait_ge(sem("r_top"), g + 1)
                    nc.vector.tensor_copy(tmp[:, 1:2], law[:, 0:1])
                    nc.vector.max_index(idx[:, :], rn[:, 0, :], ss[:, 3, :]).then_inc(sem("r_ix"), 1)
                    dve.wait_ge(sem("r_ix"), g + 1)
                    nc.vector.tensor_copy(idf[:, :], idx[:, :]).then_inc(sem("r_if"), 1)
                    dve.wait_ge(sem("r_if"), g + 1)
                    for i in range(2):
                        last = nc.vector.scalar_tensor_tensor(rn[:, 1 + i, :], const("iota"), idf[:, i:i + 1], ss[:, 2, :], ALU.is_equal, ALU.mult)
                    last.then_inc(sem("r_w"), 1)
                    dve.wait_ge(sem("r_w"), g + 1)
                    nc.vector.tensor_tensor(G[:, t, :], rn[:, 1, :], rn[:, 2, :], ALU.add).then_inc(sem("r_g"), 1)

            pipeline(dve, NT, r_body)

            acc = oT[:, 0:MT, :]
            with dve.Fori(0, NM) as m:
                for ex in range(NEX):
                    dve.wait_ge(sem("m_silu"), m * NEX + (ex + 1))
                    dve.wait_ge(sem("m_y"), m * NEX + (ex - 1 if ex >= 2 else 0))
                    nc.vector.tensor_tensor(pT[:, ex % 2, :], pj[1][:, :], e[:, 0, :], ALU.mult).then_inc(sem("m_hT"), 1)
                    dve.wait_ge(sem("m_y"), m * NEX + (ex + 1))
                    yv = sc[:, (ex % 2) * 512:(ex % 2) * 512 + 512].rearrange("p (a d) -> p a d", a=MT)
                    gt = G[:, bass.ds(m * MT, MT), min(ex, NE - 1)]
                    if ex == 0:
                        nc.vector.tensor_tensor(acc, yv, bc(gt, D), ALU.mult).then_inc(sem("m_acc"), 1)
                        continue
                    av = qn[:, ex % 2, :].rearrange("p (a d) -> p a d", a=MT)
                    if ex < NE:
                        nc.vector.tensor_tensor(av, yv, bc(gt, D), ALU.mult).then_inc(sem("m_wy"), 1)
                        dve.wait_ge(sem("m_wy"), m * (NE - 1) + ex)
                    dve.wait_ge(sem("m_acc"), m * NEX + ex)
                    nc.vector.tensor_tensor(acc, av if ex < NE else yv, acc, ALU.add).then_inc(sem("m_acc"), 1)
                dve.wait_ge(sem("m_acc"), m * NEX + NEX)
                Xm = X[:, bass.ds(m * MT, MT), :]
                nc.vector.scalar_tensor_tensor(Xm, acc, tg[:, 3:4], Xm, ALU.mult, ALU.add).then_inc(sem("m_out"), 1)

        @block.tensor
        def _(pe):
            mm = nc.tensor.matmul
            pe.wait_ge(s_ld, NLOAD)
            for i in range(2):
                if i:
                    pe.wait_ge(sem("mk_c"), i)
                for j in range(4):
                    last = nc.tensor.transpose(pt_[:, j * P:j * P + P], mkn[:, (4 * i + j) * P:(4 * i + j + 1) * P], ident)
                last.then_inc(sem("mk_T"), 1)
            pe.wait_ge(sem("mk_c"), 2)
            if stop == 0:
                return

            def x_body(a, b):
                def scores(k):
                    g, _ = b
                    pe.wait_ge(sem("x_sub"), g * 8 + (k - 1 if k >= 2 else 0))
                    s0 = (k % 2) * 512
                    for par in range(2):
                        mm(sc[:, s0 + par * 256:s0 + par * 256 + MEM], qz[:, k, par, :], mkT[:, k, :], start=True, stop=True)
                    for par in range(2):
                        for bb in range(BT):
                            r = slice(bb * 64, bb * 64 + 64)
                            last = mm(sc[r, s0 + MEM + par * S:s0 + MEM + par * S + S], qz[:, k, par, r], kT[:, k, r], start=True, stop=True)
                    last.then_inc(sem("x_s"), 1)

                def turn(k):
                    g, _ = b
                    pe.wait_ge(sem("x_p"), g * 8 + (k + 1))
                    pe.wait_ge(sem("x_ptc"), g * 8 + k)
                    for par in range(2):
                        nc.tensor.transpose(pp[:, par * P:par * P + P], e[:, k % 2, par * 256:par * 256 + MEM], ident)
                    nc.tensor.transpose(pp[:, 2 * P:3 * P], e[:, k % 2, MEM:MEM + 2 * S], ident).then_inc(sem("x_pt"), 1)

                def pv(k):
                    g, _ = b
                    pe.wait_ge(sem("x_ptc"), g * 8 + (k + 1))
                    if k % 4 == 0:
                        pe.wait_ge(sem("x_o"), g * 2 + k // 4)
                    c0 = (k % 4) * P
                    for par in range(2):
                        r = slice(par * 64, par * 64 + 64)
                        h0 = (2 * k + par) * DK
                        mm(po[0][r, c0:c0 + P], mvn[:, h0:h0 + DK], pT[:, k % 2, par * P:par * P + P], start=True, stop=False, skip_group_check=True)
                        for bb in range(BT):
                            last = mm(po[0][r, c0 + bb * 64:c0 + bb * 64 + 64], V[r, bb, k * DK:k * DK + DK],
                                      pT[r, k % 2, 2 * P + bb * 64:2 * P + bb * 64 + 64], start=False, stop=True, skip_group_check=True)
                    last.then_inc(sem("x_pv"), 1)

                def chunk(c):
                    g, _ = a
                    pe.wait_ge(sem("x_ev"), g * 6 + (c - 1 if c >= 2 else 0))
                    for j in range(4 if c < 4 else 2):
                        if c < 4:
                            blk = (c % 2) * 4 + j
                            last = mm(pj[c % 2][:, j * P:j * P + P], (xq if c < 2 else xk)[:, blk * P:blk * P + P], xcT[:, 0 if c < 2 else 1, :], start=True, stop=True)
                        else:
                            bb = c - 4
                            last = mm(pj[c % 2][j * 64:j * 64 + 64, :], xcT[:, 1, bb * 64:bb * 64 + 64],
                                      xv[:, :].rearrange("p (h a d) -> p a h d", a=2, d=DK)[:, j], start=True, stop=True)
                    last.then_inc(sem("x_proj"), 1)

                if a:
                    g, _ = a
                    pe.wait_ge(sem("x_in"), g + 1)
                    pe.wait_ge(sem("x_xcT"), g)
                    for i in range(2):
                        last = nc.tensor.transpose(pt_[:, i * P:i * P + P], xs[:, i, :], ident)
                    last.then_inc(sem("x_T"), 1)
                if b:
                    g, _ = b
                    pe.wait_ge(sem("x_ev"), g * 6 + 6)
                    scores(0)
                    scores(1)
                    for k in range(HP):
                        turn(k)
                        if k + 2 < HP:
                            scores(k + 2)
                        if k > 0:
                            pv(k - 1)
                if a:
                    g, _ = a
                    pe.wait_ge(sem("x_xcT"), g + 1)
                    for c in range(4):
                        chunk(c)
                if b:
                    pv(HP - 1)
                if a:
                    chunk(4)
                    chunk(5)
                if b:
                    g, _ = b
                    pe.wait_ge(sem("x_o"), g * 2 + 2)
                    pe.wait_ge(sem("x_res"), g)
                    for k in range(HP):
                        last = mm(po[1][:, 0:D], oT[:, k, :], xo[:, k, :], start=(k == 0), stop=(k == HP - 1))
                    last.then_inc(sem("x_wo"), 1)

            pipeline(pe, NT, x_body)
            if stop == 1:
                return
            pe.wait_ge(sem("cast"), 1)
            pe.wait_ge(sem("x_res"), NT)

            def d_body(a, b):
                def chunk(c):
                    if a:
                        g, _ = a
                        if c < 2:
                            pe.wait_ge(sem("d_v"), g * 2)
                        else:
                            pe.wait_ge(sem("d_rope"), g * 4 + (c - 1))
                        mm(pj[c % 2][:, :], xcT[:, 0, :], wqkv[:, c * 512:c * 512 + 512], start=True, stop=True).then_inc(sem("d_proj"), 1)

                def turn(c):
                    if a:
                        g, _ = a
                        pe.wait_ge(sem("d_qn"), g * 4 + (c + 1))
                        pe.wait_ge(sem("d_qkT"), g * 4 + c)
                        for j in range(4):
                            last = nc.tensor.transpose(pt_[:, j * P:j * P + P], qn[:, c % 2, j * P:j * P + P], ident)
                        last.then_inc(sem("d_TT"), 1)

                def scores(h):
                    if b:
                        g, _ = b
                        if h == 0:
                            pe.wait_ge(sem("d_qkT"), g * 4 + 4)
                        pe.wait_ge(sem("d_sub"), g * 2)
                        mm(sc[:, h * 512:h * 512 + 512], identb[:, :], bandb[:, :, :, :].rearrange("p a b t -> p (a b t)"), start=True, stop=False, skip_group_check=True)
                        for j in range(4):
                            for bb in range(BT):
                                c0 = h * 512 + (j * BT + bb) * S
                                for par in range(2):
                                    r = slice(par * 64, par * 64 + 64)
                                    last = mm(sc[r, c0:c0 + S], qT[r, 4 * h + j, bb * 64:bb * 64 + 64], kT[r, 4 * h + j, bb * 64:bb * 64 + 64], start=False, stop=True, skip_group_check=True)
                        last.then_inc(sem("d_s"), 1)

                def probsT(h):
                    if b:
                        g, _ = b
                        pe.wait_ge(sem("d_p"), g * 2 + (h + 1))
                        pe.wait_ge(sem("d_ptc"), g * 2 + h)
                        for j in range(4):
                            last = nc.tensor.transpose(pp[:, j * P:j * P + P], e[:, h, j * P:j * P + P], ident)
                        last.then_inc(sem("d_pt"), 1)

                def pv(h):
                    if b:
                        g, _ = b
                        pe.wait_ge(sem("d_ptc"), g * 2 + (h + 1))
                        pe.wait_ge(sem("d_o"), g * 2 + h)
                        pe.wait_ge(sem("d_res"), g)
                        past_waits(pe, "pe_went_on")
                        for j in range(4):
                            for par in range(2):
                                for bb in range(BT):
                                    r = slice(bb * 64, bb * 64 + 64)
                                    h0 = (2 * (4 * h + j) + par) * DK
                                    last = mm(po[bb][par * 64:par * 64 + 64, j * S:j * S + S],
                                              V[r, :, :].rearrange("p a c -> p (a c)")[:, h0:h0 + DK],
                                              pT[r, h, j * P + par * 64:j * P + par * 64 + 64], start=True, stop=True)
                        last.then_inc(sem("d_pv"), 1)

                if a:
                    g, _ = a
                    pe.wait_ge(sem("d_xin"), g + 1)
                    pe.wait_ge(sem("d_qkT"), g * 4)
                    nc.tensor.transpose(pt_[:, 0:P], xs[:, 0, :], ident).then_inc(sem("d_xT"), 1)
                scores(0)
                if a:
                    pe.wait_ge(sem("d_xsT"), a[0] + 1)
                chunk(0)
                scores(1)
                chunk(1)
                turn(0)
                probsT(0)
                chunk(2)
                turn(1)
                pv(0)
                chunk(3)
                probsT(1)
                turn(2)
                chunk(4)
                pv(1)
                turn(3)
                chunk(5)
                if b:
                    g, _ = b
                    pe.wait_ge(sem("d_o"), g * 2 + 2)
                    for k in range(HP):
                        last = mm(po[0][:, 256:256 + D], oT[:, k, :], wo[:, k, :], start=(k == 0), stop=(k == HP - 1))
                    last.then_inc(sem("d_wo"), 1)

            def f_body(a, b):
                if a:
                    g, _ = a
                    pe.wait_ge(sem("f_in"), g + 1)
                    pe.wait_ge(sem("f_xT"), g)
                    mm(pt_[:, 0:FT * 64], const("shift"), xs[:, :, 64:128], start=True, stop=True).then_inc(sem("f_sh"), 1)
                if b:
                    g, _ = b
                    pe.wait_ge(sem("f_xT"), g + 1)
                    for j, (o, n) in enumerate(FBLK):
                        pe.wait_ge(sem("f_hT"), g * 3 + (j - 1 if j >= 2 else 0))
                        for k in (1, 0):
                            last = mm(pj[j % 2][0:n, (1 - k) * 256:(1 - k) * 256 + 256], fw1[:, k * FI + o:k * FI + o + n], kT[:, 0:2, :].rearrange("p a t -> p (a t)"), start=True, stop=True)
                        last.then_inc(sem("f_h"), 1)
                if a:
                    g, _ = a
                    pe.wait_ge(sem("f_xn"), g + 1)
                    for i in range(FT):
                        last = nc.tensor.transpose(pt_[:, i * P:i * P + P], qn[:, 0, i * P:i * P + P], ident)
                    last.then_inc(sem("f_xnT"), 1)
                if b:
                    g, _ = b
                    pe.wait_ge(sem("y_ready"), g * FT + NT)
                    for i in range(FT):
                        mm(sc[:, i * D:i * D + D], const("ones")[0:1, :], fb2[:, :], start=True, stop=False)
                        for j, (o, n) in enumerate(FBLK):
                            if i == 0:
                                pe.wait_ge(sem("f_hT"), g * 3 + (j + 1))
                            last = mm(sc[:, i * D:i * D + D], big2[0:n, j * 256 + i * P:j * 256 + i * P + P], fw2[0:n, j, :], start=False, stop=(j == 2))
                    last.then_inc(sem("f_y"), 1)

            with pe.Fori(0, layers) as l:
                pe.wait_ge(sem("att_loaded"), l * ATT_LOADS + ATT_LOADS)
                pe.wait_ge(sem("f_xT"), l * NF)
                pe.wait_ge(sem("f_xn"), l * NF)
                pe.wait_ge(sem("f_hT"), l * (3 * NF))
                pe.wait_ge(sem("y_ready"), l * NT + NT)
                pipeline(pe, NT, d_body, l * NT)
                pe.wait_ge(sem("ffn_loaded"), l * FFN_LOADS + FFN_LOADS)
                pe.wait_ge(sem("d_v"), l * (2 * NT) + 2 * NT)
                pe.wait_ge(sem("d_qkT"), l * (4 * NT) + 4 * NT)
                pe.wait_ge(sem("d_sub"), l * (2 * NT) + 2 * NT)
                pipeline(pe, NF, f_body, l * NF)
            if stop == 2:
                return

            def l_body(a, b):
                if a:
                    g, _ = a
                    pe.wait_ge(sem("l_in"), g + 1)
                    pe.wait_ge(sem("l_xcT"), g)
                    for i in range(2):
                        last = nc.tensor.transpose(pt_[:, i * P:i * P + P], xs[:, i, :], ident)
                    last.then_inc(sem("l_T"), 1)
                if b:
                    g, _ = b
                    pe.wait_ge(sem("l_km"), g + 1)
                    pe.wait_ge(sem("l_V"), g + 1)
                    pe.wait_ge(sem("l_sub"), g)
                    km = big[:, :, :, :, :].rearrange("p w h a t -> p w (h a) t")
                    for hh in range(2):
                        for bb in range(BT):
                            r = slice(bb * 64, bb * 64 + 64)
                            last = mm(sc[r, hh * 512:hh * 512 + 512], kT[:, 1, r], km[:, bb, 8 * hh:8 * hh + 8, 0:S], start=True, stop=True)
                    last.then_inc(sem("l_s"), 1)
                if a:
                    g, _ = a
                    pe.wait_ge(sem("l_xcT"), g + 1)
                    pe.wait_ge(sem("l_V"), g)
                    mm(pj[0][:, 0:P], lq[:, :], xcT[:, 0, :], start=True, stop=True)
                    mm(pj[0][:, P:2 * P], lkv[:, 0:D], xcT[:, 1, :], start=True, stop=True)
                    mm(pj[0][0:L1H, 2 * P:3 * P], lla[:, :], xcT[:, 1, :], start=True, stop=True)
                    vv = lkv[:, D:2 * D].rearrange("p (h a d) -> p a h d", a=2, d=L1D)
                    for bb in range(BT):
                        for par in range(2):
                            last = mm(pj[0][par * 64:par * 64 + 64, 3 * P + bb * 64:3 * P + bb * 64 + 64], xcT[:, 1, bb * 64:bb * 64 + 64], vv[:, par], start=True, stop=True)
                    last.then_inc(sem("l_proj"), 1)
                if b:
                    g, _ = b
                    for h in range(2):
                        if h == 0:
                            pe.wait_ge(sem("l_p"), g + 1)
                        pe.wait_ge(sem("l_ptc"), g * 2 + h)
                        for j in range(4):
                            last = nc.tensor.transpose(pp[:, j * P:j * P + P], e[:, h, j * P:j * P + P], ident)
                        last.then_inc(sem("l_pt"), 1)
                    pe.wait_ge(sem("l_ptc"), g * 2 + 2)
                    pe.wait_ge(sem("l_res"), g)
                    past_waits(pe, "pe_went_on")
                    for k in range(HP):
                        for bb in range(BT):
                            for par in range(2):
                                r = slice(par * 64, par * 64 + 64)
                                c = bb * 64 + k * L1D
                                last = mm(po[par][bb * 64:bb * 64 + 64, k * L1D:k * L1D + L1D], pT[r, k // 4, (k % 4) * P + bb * 64:(k % 4) * P + bb * 64 + 64],
                                          V[r, 0, c:c + L1D], start=True, stop=True)
                    last.then_inc(sem("l_pv"), 1)
                    pe.wait_ge(sem("l_o"), g + 1)
                    nc.tensor.transpose(po[0][:, P:2 * P], tmp[:, :], ident).then_inc(sem("l_oT"), 1)
                    pe.wait_ge(sem("l_oTc"), g + 1)
                    mm(po[1][:, P:2 * P], oT[:, 0, :], lpj[:, :], start=True, stop=True).then_inc(sem("l_pr"), 1)
                if a:
                    g, _ = a
                    pe.wait_ge(sem("l_gb"), g + 1)
                    pe.wait_ge(sem("l_c1"), g)
                    mm(pt_[:, 2 * P:2 * P + L1H], gb_ap, ident[0:L1H, 0:L1H], start=True, stop=True).then_inc(sem("l_gr"), 1)

            gb_ap = qn[0:L1H, 0, 0:P]
            pe.wait_ge(sem("n_y"), 3)
            pipeline(pe, NT, l_body)
            if stop == 3:
                return
            pe.wait_ge(sem("exp_loaded"), 6 * 16)
            pe.wait_ge(sem("l_res"), NT)
            for i, some in enumerate(TURN4):
                if i:
                    pe.wait_ge(sem("w_c"), i)
                for j, (k, ex) in enumerate(some):
                    last = nc.tensor.transpose(pt_[:, j * P:j * P + P], expert_natural(k, ex), ident)
                last.then_inc(sem("w_T"), 1)
            nc.tensor.transpose(pp[:, 0:NE], egw[:, :], ident[0:NE, 0:NE]).then_inc(sem("g_T"), 1)
            pe.wait_ge(sem("g_c"), 1)
            pe.wait_ge(sem("w_c"), len(TURN4))

            def r_body(a, b):
                if a:
                    g, _ = a
                    pe.wait_ge(sem("r_in"), g + 1)
                    pe.wait_ge(sem("r_xT"), g)
                    nc.tensor.transpose(pt_[:, 0:P], xs[:, 0, :], ident).then_inc(sem("r_T"), 1)
                    pe.wait_ge(sem("r_XT"), g + 1)
                    pe.wait_ge(sem("r_mx"), g)
                    mm(pp[:, 0:NE], xcT[:, 0, :], egT[:, :], start=True, stop=True).then_inc(sem("r_lg"), 1)

            pipeline(pe, NT, r_body)

            with pe.Fori(0, NM) as m:
                def up(ex):
                    pe.wait_ge(sem("m_hT"), m * NEX + ex)
                    rows = CT[:, bass.ds(m * MT, MT), :].rearrange("p a t -> p (a t)")
                    mm(pj[0][:, :], expert_T(1, ex), rows, start=True, stop=True)
                    mm(pj[1][:, :], expert_T(3, ex), rows, start=True, stop=True).then_inc(sem("m_h"), 1)

                def down(ex):
                    pe.wait_ge(sem("m_hT"), m * NEX + (ex + 1))
                    pe.wait_ge(sem("m_acc"), m * NEX + (ex - 1 if ex >= 2 else 0))
                    for j in range(MT):
                        last = mm(sc[:, (ex % 2) * 512 + j * P:(ex % 2) * 512 + j * P + P], pT[:, ex % 2, j * P:j * P + P], expert_T(2, ex), start=True, stop=True)
                    last.then_inc(sem("m_y"), 1)

                for ex in range(NEX):
                    up(ex)
                    down(ex)


_INS = ['x', 'ctx_1024', 'g_xattn', 'g_ffn', 'L0_xattn_wq_w', 'L0_xattn_wq_b', 'L0_xattn_wk_w', 'L0_xattn_wk_b',
        'L0_xattn_wv_w', 'L0_xattn_wv_b', 'L0_xattn_mk', 'L0_xattn_mv', 'L0_xattn_wo_w', 'L0_xattn_wo_b',
        'L0_ffn_Wqkv', 'L0_ffn_q_scale', 'L0_ffn_k_scale', 'L0_ffn_Wo', 'L0_ffn_ln_g', 'L0_ffn_ln_b', 'L0_ffn_W1',
        'L0_ffn_b1', 'L0_ffn_W2', 'L0_ffn_b2', 'L1_xattn_w_kv', 'L1_xattn_w_q', 'L1_xattn_w_la', 'L1_xattn_w_proj',
        'L1_xattn_b_proj', 'L1_xattn_att_weight', 'L1_ffn_gate_w', 'L1_ffn_gate_bias', 'L1_ffn_w1', 'L1_ffn_w3',
        'L1_ffn_w2', 'L1_ffn_sw1', 'L1_ffn_sw3', 'L1_ffn_sw2']


def shape_constants():
    import numpy as np
    f = np.float32
    k = np.zeros((P, NCONST), f)

    def put(name, a):
        o, n = CONSTS[name]
        k[:, o:o + n] = a

    put("ident", np.eye(P, dtype=f))
    shift = np.zeros((P, P), f)
    for m in range(P):
        if m % S:
            shift[m - 1, m] = 1.0
    put("shift", shift)
    half = np.arange(0, DK, 2, dtype=f)
    inv_freq = f(1.0) / np.power(f(10000.0), half / f(DK))
    t = np.arange(S, dtype=f)
    freqs = np.concatenate([t[:, None] * inv_freq[None, :]] * 2, -1)
    base = (half + f(0.4 * DK)) / f(1.4 * DK)
    power = (t - S // 2) / f(WINDOW // 2)
    scale = np.concatenate([np.power(base[None, :], power[:, None])] * 2, -1)
    sign = np.where(np.arange(DK) < DK // 2, f(-1), f(1))
    for name, sc in (("q", scale), ("k", f(1.0) / scale)):
        put(name + "cos", np.tile(np.cos(freqs) * sc, (BT, 1)))
        put(name + "sin", np.tile(np.sin(freqs) * sc * sign, (BT, 1)))
    i, j = np.arange(S)[:, None], np.arange(S)[None, :]
    put("band", np.tile(np.where((i < j) | (i > j + WINDOW), f(MASKED), f(0)), (BT, 1)))
    put("iota", np.arange(NE, dtype=f)[None, :])
    put("headmask", (np.arange(P)[:, None] // L1D == np.arange(L1H)[None, :]).astype(f))
    put("half", f(-0.5))
    put("eps", f(EPS))
    put("ones", f(1.0))
    return k


def kernel(**inputs):
    import numpy as np
    import concourse.bacc as bacc
    from concourse.bass_utils import run_bass_kernel_spmd

    nc = bacc.Bacc("TRN2", target_bir_lowering=False, num_devices=1)
    arrays, args = {}, []
    for name in _INS + ["consts"]:
        a = shape_constants() if name == "consts" else np.ascontiguousarray(inputs[name])
        arrays[f"in_{name}"] = a
        args.append(nc.dram_tensor(f"in_{name}", a.shape, mybir.dt.from_np(a.dtype), kind="ExternalInput").ap())
    args.append(nc.dram_tensor("out_x", (B, S, D), F32, kind="ExternalOutput").ap())
    build(nc, *args)
    r = run_bass_kernel_spmd(nc, [arrays], core_ids=[0])
    return r.results[0]["out_x"]
```

```python
from contextlib import ExitStack

import concourse.bass as bass
from concourse import mybir

P = 128
B, S, D = 64, 64, 128
BT = P // S
NT = B // BT
H, DK = 16, 64
HP = H // 2
INNER = H * DK
MEM = 128
DEPTH = 6
WINDOW = 32
FI = int(D * 4 * 2 / 3)
FBLK = [(0, P), (P, P), (2 * P, FI - 2 * P)]
FT = 2
NF = NT // FT
L1H, L1D = 16, 8
NE = 8
NEX = NE + 2
MT = 4
NM = NT // MT
NB = 8
QK_SCALE = 8.0
MASKED = -1e30
EPS = 1e-5

ALU = mybir.AluOpType
ACT = mybir.ActivationFunctionType
F32 = mybir.dt.float32
BF16 = mybir.dt.bfloat16
U32 = mybir.dt.uint32
I32 = mybir.dt.int32
AX = mybir.AxisListType.X

CONSTS = {}
_at = 0
for _name, _n in (("ident", P), ("shift", P), ("qcos", DK), ("kcos", DK), ("qsin", DK), ("ksin", DK),
                  ("band", DK), ("iota", NE), ("headmask", L1H // 2), ("half", NT), ("eps", 4), ("threehalves", 32), ("ones", P)):
    CONSTS[_name] = (_at, _n)
    _at += _n
NCONST = _at


def build(nc, x, ctx, g_xattn, g_ffn, wq_w, wq_b, wk_w, wk_b, wv_w, wv_b, mk, mv, wo_w, wo_b,
          Wqkv, q_scale, k_scale, Wo, ln_g, ln_b, W1, b1, W2, b2,
          w_kv, w_q, w_la, w_proj, b_proj, att_weight,
          gate_w, gate_bias, w1, w3, w2, sw1, sw3, sw2, consts, out):
    with ExitStack() as stack:
        def sb(name, shape, dt=F32):
            return stack.enter_context(nc.sbuf_tensor(name, shape, dt))

        sems = {}

        def sem(name):
            if name not in sems:
                sems[name] = stack.enter_context(nc.semaphore(name))
            return sems[name]

        X = sb("X", [P, NT, D])
        Y = sb("Y", [P, NT, D])
        CT = sb("CT", [P, NT, D])
        K = sb("K", [P, NCONST])

        def const(name):
            a, n = CONSTS[name]
            return K[:, a:a + n]

        ident = const("ident")
        identb = sb("identb", [P, P], BF16)
        bandb = sb("bandb", [P, 4, BT, S], BF16)
        gates = sb("gates", [P, 4])
        tg = sb("tg", [P, 4])
        st = sb("st", [P, NT, 6])
        mean = sb("mean", [P, NT])
        dif = sb("dif", [P, NT])
        var = sb("var", [P, NT])
        m2 = sb("m2", [P, NT])
        rstd = sb("rstd", [P, NT])
        nhalf = const("half")

        xq = sb("xq", [P, INNER])
        xk = sb("xk", [P, INNER])
        xv = sb("xv", [P, INNER])
        xo = sb("xo", [P, HP, D])
        mkn = sb("mkn", [P, INNER])
        mkT = sb("mkT", [P, HP, MEM])
        mvn = sb("mvn", [P, INNER])
        qb = sb("qb", [P, HP])
        kb = sb("kb", [P, HP])
        vb = sb("vb", [P, HP, DK])
        ob = sb("ob", [P, D])
        wqkv = sb("wqkv", [P, 3 * INNER])
        wo = sb("wo", [P, HP, D])
        qs = sb("qs", [P, 2, DK])
        rc_ = sb("ropec", [P, 2, DK])
        rs_ = sb("ropes", [P, 2, DK])
        fw1 = sb("fw1", [P, 2 * FI])
        fw2 = sb("fw2", [P, 3, D])
        fg = sb("fg", [P, 2])
        fb1 = sb("fb1", [P, 2, 3])
        fb2 = sb("fb2", [1, D])
        lkv = sb("lkv", [P, 2 * D])
        lq = sb("lq", [P, D])
        lla = sb("lla", [P, L1H])
        lpj = sb("lpj", [P, D])
        lpb = sb("lpb", [P, D])
        law = sb("law", [P, 2])
        egw = sb("egw", [NE, D])
        egT = sb("egT", [P, NE])
        egb = sb("egb", [P, NE])
        G = sb("G", [P, NT, NE])
        GR = sb("GR", [P, NT, L1H])

        xs = sb("xs", [P, 2, D])
        xcT = sb("xcT", [P, 2, P])
        big = sb("big", [P, 2, HP, 2, P])
        kT = sb("kT", [P, HP, P])
        V = sb("V", [P, 2, HP * DK])
        e = sb("e", [P, 4, 512])
        pT = sb("pT", [P, 2, 512])
        oT = sb("oT", [P, HP, P])
        mx = sb("mx", [P, 2, 16])
        sm = sb("sm", [P, 2, 16])
        rc = sb("rc", [P, 2, 16])
        tmp = sb("tmp", [P, D])
        ss = sb("ss", [P, 4, 8])
        rn = sb("rn", [P, 4, 8])

        pj = [stack.enter_context(nc.psum_tensor(f"pj{i}", [P, 512], F32)) for i in range(2)]
        pt_ = stack.enter_context(nc.psum_tensor("turn", [P, 512], F32))
        sc = stack.enter_context(nc.psum_tensor("sc", [P, 1024], F32))
        pp = stack.enter_context(nc.psum_tensor("pp", [P, 512], F32))
        po = [stack.enter_context(nc.psum_tensor(f"po{i}", [P, 512], F32)) for i in range(2)]

        qz = big[:, 0]
        bq = big[:, :, :, :, :].rearrange("p w h a t -> p (w h a t)")
        qT = bq[:, 0:1024].rearrange("p (h t) -> p h t", h=HP)
        U = [bq[:, 1024 + 512 * i:1536 + 512 * i] for i in range(4)]
        t2b = [bq[:, 3072 + 512 * i:3584 + 512 * i] for i in range(2)]
        qn = sb("qn", [P, 4, 512])
        big2 = sb("big2", [P, 1024])
        sqb = [big2[:, 0:512], big2[:, 512:1024]]
        xp = sb("xp", [P, P])
        ssc = sb("ssc", [P, 32])
        xh = sb("xh", [P, 32])
        ny = sb("ny", [P, 2, 32])

        xd = x.rearrange("b s d -> (b s) d").rearrange("(i p) d -> p i d", p=P)
        cd = ctx.rearrange("b s d -> (b s) d").rearrange("(i p) d -> p i d", p=P)
        od = out.rearrange("b s d -> (b s) d").rearrange("(i p) d -> p i d", p=P)

        def bc(ap, n):
            return ap.unsqueeze(len(ap.shape)).broadcast_to(list(ap.shape) + [n])

        def pbc(ap, n=P):
            return ap.partition_broadcast(n)

        s_ld = sem("loaded")
        loads = [0]

        ATT_LOADS = 4 * 16
        FFN_LOADS = (2 + 1 + 2 + 3 * 2 + 1) * 16

        wst1, wst3, wst2 = (w[:, :].rearrange("p (e d) -> p e d", e=NE) for w in (xq, xk, xv))
        sst = wqkv[:, 0:6 * P].rearrange("p (k e d) -> p k e d", k=3, e=2)
        eT = {1: mkn[:, :].rearrange("p (e d) -> p e d", e=NE), 3: mvn[:, :].rearrange("p (e d) -> p e d", e=NE),
              2: mkT[:, :, :]}
        sT = wqkv[:, 6 * P:12 * P].rearrange("p (k e d) -> p k e d", k=3, e=2)

        def expert_T(k, ex):
            return eT[k][:, ex, :] if ex < NE else sT[:, (1, 3, 2).index(k), ex - NE, :]

        def expert_natural(k, ex):
            return (dict(zip((1, 3, 2), (wst1, wst3, wst2)))[k][:, ex, :] if ex < NE
                    else sst[:, (1, 3, 2).index(k), ex - NE, :])

        TURNS = [(k, ex) for k in (1, 3, 2) for ex in range(NEX)]
        TURN4 = [TURNS[i:i + 4] for i in range(0, len(TURNS), 4)]

        L1HALF = L1H // 2

        l_e1 = [e[:, h, :].rearrange("p (j t) -> p j t", t=S) for h in range(2)]
        l_zb = [big2[:, 512 * h:512 * h + 512].rearrange("p (j t) -> p j t", t=S) for h in range(2)]
        l_mb = [qn[:, h, :].rearrange("p (j t) -> p j t", t=S) for h in range(2)]
        l_pb = [e[:, 2 + h, :].rearrange("p (j t) -> p j t", t=S) for h in range(2)]
        l_km = bq[:, 0:BT * 512].rearrange("p (b j t) -> p b j t", b=BT, t=S)
        l_vp = V[:, 0, 0:2 * P].rearrange("p (b k a d) -> p b k a d", b=BT, a=2, d=L1D)
        l_gm = ss[0:L1H, 0, :]
        l_gb = qn[0:L1H, 2, 0:P]

        def h8(buf, i, h):
            return buf[:, i, L1HALF * h:L1HALF * h + L1HALF]

        h_banks = [pj, [pt_, pp]]

        block = stack.enter_context(nc.Block())

        def past_waits(eng, name):
            eng.sem_inc(sem(name), 1)

        def reaches(eng, name, count):
            if not (isinstance(count, int) and count <= 0):
                eng.wait_ge(sem(name), count)

        def pipeline(eng, n, body, base=0, stages=2):
            def tile(k):
                return base + k, k

            for k in range(stages - 1):
                body(*(tile(k - s) if s <= k else None for s in range(stages)))
            rounds = (n - stages + 1) // 2
            with eng.Fori(0, rounds) as i:
                for k in range(stages - 1, stages + 1):
                    body(*((i * 2 + base + (k - s), i * 2 + (k - s)) for s in range(stages)))
            for k in range(stages - 1 + 2 * rounds, n + stages - 1):
                body(*(tile(k - s) if k - s < n else None for s in range(stages)))

        @block.sync
        def _(sp):
            def load(dst, src):
                sp.dma_start(dst, src, allow_slow_non_contiguous=True).then_inc(s_ld, 16)

            load(K[:, :], consts)
            load(X[:, :, :], xd)
            load(CT[:, :, :], cd)
            load(xq[:, :], wq_w)
            load(xk[:, :], wk_w)
            load(xv[:, :], wv_w)
            load(mkn[:, :], mk.rearrange("a m n -> (a m) n"))
            load(mvn[:, :], mv.rearrange("a m n -> (a m) n"))
            load(xo[:, :, :], wo_w.rearrange("(c p) n -> p c n", p=P))
            load(qb[:, :], wq_b.rearrange("(c p) -> p c", p=P))
            load(kb[:, :], wk_b.rearrange("(c p) -> p c", p=P))
            for par in range(2):
                load(vb[par * 64:par * 64 + 64, :, :],
                     pbc(wv_b.rearrange("(h a d) -> a h d", a=2, d=DK)[par], 64))
            load(ob[:, :], pbc(wo_b))
            load(gates[:, 0:1], pbc(g_xattn[0:1]))
            load(gates[:, 1:2], pbc(g_ffn[0:1]))
            load(gates[:, 2:3], pbc(g_xattn[1:2]))
            load(gates[:, 3:4], pbc(g_ffn[1:2]))
            load(lkv[:, :], w_kv)
            load(lq[:, :], w_q)
            load(lla[:, :], w_la)
            load(lpj[:, :], w_proj)
            load(lpb[:, :], pbc(b_proj))
            load(law[:, 0:1], pbc(att_weight))
            load(egw[:, :], gate_w)
            load(egb[:, :], pbc(gate_bias))

            with sp.Fori(0, DEPTH) as l:
                sp.wait_ge(sem("d_wo"), l * NT)
                sp.dma_start(wqkv[:, :], Wqkv[l, :, :]).then_inc(sem("att_loaded"), 16)
                sp.dma_start(wo[:, :, :], Wo[l, :, :].rearrange("(c p) n -> p c n", p=P)).then_inc(sem("att_loaded"), 16)
                sp.dma_start(qs[:, 0, :], pbc(q_scale[l, :])).then_inc(sem("att_loaded"), 16)
                sp.dma_start(qs[:, 1, :], pbc(k_scale[l, :])).then_inc(sem("att_loaded"), 16)
                sp.wait_ge(sem("f_res"), l * NF)

                def fload(dst, src):
                    sp.dma_start(dst, src, allow_slow_non_contiguous=True).then_inc(sem("ffn_loaded"), 16)

                fload(fw1[:, :], W1[l, :, :])
                fload(fw2[:, 0:2, :], W2[l, 0:2 * P, :].rearrange("(c p) n -> p c n", p=P))
                fload(fw2[0:FI - 2 * P, 2, :], W2[l, 2 * P:FI, :])
                fload(fg[:, 0:1], ln_g[l, :].rearrange("(p a) -> p a", a=1))
                fload(fg[:, 1:2], ln_b[l, :].rearrange("(p a) -> p a", a=1))
                for k in range(2):
                    for j, (o, n) in enumerate(FBLK):
                        fload(fb1[0:n, k, j:j + 1], b1[l, k * FI + o:k * FI + o + n].rearrange("(p a) -> p a", a=1))
                fload(fb2[:, :], b2[l, :].rearrange("(a n) -> a n", a=1))
            sp.wait_ge(sem("d_wo"), DEPTH * NT)
            for wst, src in ((wst1, w1), (wst3, w3), (wst2, w2)):
                sp.dma_start(wst, src.rearrange("e i d -> i e d")).then_inc(sem("exp_loaded"), 16)
            for i, src in enumerate((sw1, sw3)):
                sp.dma_start(sst[:, i, :, :], src.rearrange("(e i) d -> i e d", e=2)).then_inc(sem("exp_loaded"), 16)
            sp.dma_start(sst[:, 2, :, :], sw2.rearrange("d (e i) -> d e i", e=2)).then_inc(sem("exp_loaded"), 16)
            for m in range(NM):
                sp.wait_ge(sem("m_out"), m + 1)
                sp.dma_start(od[:, m * MT:m * MT + MT, :], X[:, m * MT:m * MT + MT, :]).then_inc(sem("stored"), 16)
            sp.wait_ge(sem("stored"), 16 * NM)
        NLOAD = 26 * 16

        @block.gpsimd
        def _(pool):
            def rsqrt_many(n):
                pool.wait_ge(sem("n_var"), n)
                nc.gpsimd.tensor_scalar(var[:, :], var[:, :], EPS, None, ALU.add).then_inc(sem("n_eps"), 1)
                pool.wait_ge(sem("n_eps"), n)
                nc.gpsimd.tensor_tensor(rstd[:, :], var[:, :], nhalf, ALU.pow).then_inc(sem("n_rstd"), 1)

            def feed(pre, n_in, n_used):
                def f(g, t):
                    pool.wait_ge(sem(n_used), g)
                    nc.gpsimd.tensor_copy(xs[:, 0, :], Y[:, t, :])
                    nc.gpsimd.tensor_copy(xs[:, 1, :], CT[:, t, :]).then_inc(sem(n_in), 1)
                return f

            pool.wait_ge(s_ld, NLOAD)
            nc.gpsimd.memset(big[:, 0, :, :, :], 0.0).then_inc(sem("zeroed"), 1)
            rsqrt_many(1)
            pool.wait_ge(sem("n_y"), 1)
            copy_in = feed("x", "x_in", "x_T")

            def x_body(a, b, c):
                def probs(n, k):
                    pool.wait_ge(sem("x_rc"), n)
                    pool.wait_ge(sem("x_e"), n)
                    ev = e[:, k % 4, 0:384].rearrange("p (a t) -> p a t", a=2)
                    nc.gpsimd.tensor_tensor(ev, ev, bc(rc[:, k % 2, 0:2], 192), ALU.mult).then_inc(sem("x_p"), 1)

                if c:
                    probs(c[0] * 8 + 8, 7)
                if a:
                    copy_in(*a)
                if b:
                    for k in range(HP - 1):
                        probs(b[0] * 8 + (k + 1), k)

            pipeline(pool, NT, x_body, 0, 3)
            rsqrt_many(2)
            pool.wait_ge(sem("n_y"), 2)
            nc.gpsimd.memset(xcT[:, 0, :], 0.0).then_inc(sem("zeroed"), 1)

            def d_body(n, a, b, c, d):
                if b:
                    g, _ = b
                    for i in (2, 3):
                        pool.wait_ge(sem("d_newton"), g * 12 + 12)
                        pool.wait_ge(sem("d_u"), g * 4 + (i + 1))
                        pool.wait_ge(sem("d_TT"), g * 4)
                        nc.gpsimd.tensor_tensor(qn[:, i, :].rearrange("p (h d) -> p h d", d=DK),
                                                U[i].rearrange("p (h d) -> p h d", d=DK), bc(ny[:, 0, 8 * i:8 * i + 8], DK), ALU.mult).then_inc(sem("d_kn"), 1)
                if a:
                    g, _ = a
                    for i in range(4):
                        pool.wait_ge(sem("d_rope"), g * 4 + (i + 1))
                        nc.gpsimd.tensor_tensor(U[i], U[i], t2b[i % 2], ALU.add).then_inc(sem("d_u"), 1)
                    y, w = ny[:, 0, :], ny[:, 1, :]
                    pool.wait_ge(sem("d_xh"), g + 1)
                    pool.wait_ge(sem("d_qn"), g * 2)
                    for i in range(3):
                        for j, (o, p, q, op) in enumerate(((w, y, y, ALU.mult), (w, w, xh[:, :], ALU.mult),
                                                           (w, w, const("threehalves"), ALU.add), (y, y, w, ALU.mult))):
                            if i + j:
                                pool.wait_ge(sem("d_newton"), g * 12 + (4 * i + j))
                            last = nc.gpsimd.tensor_tensor(o, p, q, op).then_inc(sem("d_newton"), 1)
                if b:
                    g, _ = b
                    for h in range(2):
                        pool.wait_ge(sem("d_rc"), g * 2 + (h + 1))
                        ev = e[:, h, :].rearrange("p (a t) -> p a t", t=S)
                        nc.gpsimd.tensor_tensor(ev, ev, bc(rc[:, h, 0:8], S), ALU.mult).then_inc(sem("d_p"), 1)

            def f_body(a, b, c):
                if a:
                    g, t = a
                    pool.wait_ge(sem("f_mv"), g + 1)
                    nc.gpsimd.tensor_tensor(m2[:, 0:FT], var[:, 0:FT], const("eps")[:, 0:FT], ALU.add).then_inc(sem("f_eps"), 1)
                    pool.wait_ge(sem("f_eps"), g + 1)
                    pool.wait_ge(sem("f_xn"), g)
                    nc.gpsimd.tensor_tensor(rstd[:, 0:FT], m2[:, 0:FT], nhalf[:, 0:FT], ALU.pow).then_inc(sem("f_rstd"), 1)

            with pool.Fori(0, DEPTH) as l:
                pipeline(pool, NT, d_body, l * NT, 5)
                pipeline(pool, NF, f_body, l * NF, 3)
            rsqrt_many(3)
            pool.wait_ge(sem("n_y"), 3)

            def l_body(n, a, b, c, d):
                def second(g, h):
                    u = g * 2 + h
                    pool.wait_ge(sem("l_c1"), u + 1)
                    reaches(pool, "l_p", u - 1)
                    nc.gpsimd.tensor_tensor(l_zb[h], l_e1[h], bc(h8(rc, 1, h), S), ALU.mult).then_inc(sem("l_z"), 1)

                def first(g, h):
                    nc.gpsimd.tensor_tensor(l_mb[h], l_e1[h], bc(h8(sm, 1, h), S), ALU.mult).then_inc(sem("l_m1"), 1)

                def mixture(g, h):
                    u = g * 2 + h
                    pool.wait_ge(sem("l_m2"), u + 1)
                    pool.wait_ge(sem("l_m1"), u + 1)
                    reaches(pool, "l_pt", u - 1)
                    nc.gpsimd.tensor_tensor(l_pb[h], l_mb[h], l_zb[h], ALU.add).then_inc(sem("l_p"), 1)

                if a:
                    g, _ = a
                    pool.wait_ge(sem("l_kT"), g + 1)
                    reaches(pool, "l_s", g * 2)
                    kk = kT[:, 0, :].rearrange("p (b t) -> p b t", b=BT)
                    for bb in range(BT):
                        last = nc.gpsimd.tensor_tensor(
                            l_km[:, bb], kk[:, bb, :].unsqueeze(1).broadcast_to([P, L1HALF, S]),
                            bc(const("headmask"), S), ALU.mult)
                    last.then_inc(sem("l_km"), 1)
                if b:
                    second(b[0], 0)
                if c:
                    mixture(c[0], 1)
                if b:
                    first(b[0], 0)
                if b:
                    second(b[0], 1)
                    mixture(b[0], 0)
                    first(b[0], 1)

            nc.gpsimd.memset(V[:, 0, 0:2 * P], 0.0).then_inc(sem("zeroed"), 1)
            pipeline(pool, NT, l_body, 0, 5)
            rsqrt_many(4)
            pool.wait_ge(sem("n_y"), 4)

            def r_body(a, b):
                if a:
                    g, t = a
                    pool.wait_ge(sem("r_T"), g)
                    nc.gpsimd.tensor_copy(xs[:, 0, :], Y[:, t, :]).then_inc(sem("r_in"), 1)

            pipeline(pool, NT, r_body)

        @block.scalar
        def _(act):
            act.wait_ge(s_ld, NLOAD)
            nc.scalar.activation(tg[:, :], gates[:, :], ACT.Tanh).then_inc(sem("tanh"), 1)
            nc.scalar.copy(identb[:, :], ident)
            for i in range(4 * BT):
                last = nc.scalar.copy(bandb[:, i // BT, i % BT, :], const("band"))
            last.then_inc(sem("cast"), 1)
            for i in range(2):
                act.wait_ge(sem("mk_T"), i + 1)
                nc.scalar.copy(mkT[:, 4 * i:4 * i + 4, :].rearrange("p h m -> p (h m)"), pt_[:, :]).then_inc(sem("mk_c"), 1)

            def x_body(a, b, c):
                def turned(n, j):
                    act.wait_ge(sem("x_pt"), n)
                    reaches(act, "x_pv", n - 2)
                    nc.scalar.copy(pT[:, j % 2, 0:384], pp[:, 0:384]).then_inc(sem("x_ptc"), 1)

                def heads_out(g, half):
                    act.wait_ge(sem("x_pv"), g * 8 + (4 * half + 4))
                    reaches(act, "x_wo", g)
                    nc.scalar.copy(oT[:, 4 * half:4 * half + 4, :].rearrange("p h t -> p (h t)"), po[0][:, :]).then_inc(sem("x_o"), 1)

                for k in range(HP):
                    if b:
                        act.wait_ge(sem("x_sub"), b[0] * 8 + (k + 1))
                        nc.scalar.activation(e[:, k % 4, 0:384], e[:, k % 4, 0:384], ACT.Exp, scale=DK ** -0.5).then_inc(sem("x_e"), 1)
                    if k < 2:
                        if c:
                            turned(c[0] * 8 + (k + 7), k + 6)
                    elif b:
                        turned(b[0] * 8 + (k - 1), k - 2)
                    if k == 2 and c:
                        heads_out(c[0], 1)
                    if k == 3 and a:
                        g, _ = a
                        act.wait_ge(sem("x_T"), g + 1)
                        reaches(act, "x_proj", g * 6)
                        nc.scalar.copy(xcT[:, :, :].rearrange("p a t -> p (a t)"), pt_[:, 0:2 * P]).then_inc(sem("x_xcT"), 1)
                    if k == 6 and b:
                        heads_out(b[0], 0)

            pipeline(act, NT, x_body, 0, 3)
            act.wait_ge(sem("zeroed"), 2)

            def d_body(n, a, b, c, d):
                def square(i):
                    if a:
                        g, _ = a
                        act.wait_ge(sem("d_proj"), g * 4 + (i + 1))
                        act.wait_ge(sem("d_ss"), g * 4 + (i - 1 if i >= 2 else 0))
                        nc.scalar.activation(sqb[i % 2], pj[i % 2][:, :], ACT.Square).then_inc(sem("d_sq"), 1)

                def turned(i):
                    if b:
                        g, _ = b
                        act.wait_ge(sem("d_TT"), g * 4 + (i + 1))
                        act.wait_ge(sem("d_s"), g * 2)
                        dst = (qT if i < 2 else kT)[:, (i % 2) * 4:(i % 2) * 4 + 4, :]
                        nc.scalar.copy(dst.rearrange("p h t -> p (h t)"), pt_[:, :]).then_inc(sem("d_qkT"), 1)

                def exps(h):
                    if b:
                        g, _ = b
                        act.wait_ge(sem("d_sub"), g * 2 + (h + 1))
                        nc.scalar.activation(e[:, h, :], e[:, h, :], ACT.Exp, scale=QK_SCALE).then_inc(sem("d_e"), 1)

                def values(i):
                    if b:
                        g, _ = b
                        act.wait_ge(sem("d_vproj"), g * 2 + (i + 1))
                        act.wait_ge(sem("d_pv"), g * 2)
                        nc.scalar.copy(V[:, i, :], pj[i][:, :]).then_inc(sem("d_v"), 1)

                def probsT(h):
                    if c:
                        g, _ = c
                        act.wait_ge(sem("d_pt"), g * 2 + (h + 1))
                        act.wait_ge(sem("d_pv"), g * 2)
                        nc.scalar.copy(pT[:, h, :], pp[:, :]).then_inc(sem("d_ptc"), 1)

                def outT(h):
                    if c:
                        g, _ = c
                        act.wait_ge(sem("d_pv"), g * 2 + (h + 1))
                        act.wait_ge(sem("d_wo"), g)
                        ov = oT[:, 4 * h:4 * h + 4, :].rearrange("p h (b s) -> p h b s", b=BT)
                        for bb in range(BT):
                            last = nc.scalar.copy(ov[:, :, bb, :], po[bb][:, 0:256].rearrange("p (h s) -> p h s", h=4))
                        last.then_inc(sem("d_o"), 1)

                square(0)
                square(1)
                turned(0)
                probsT(0)
                turned(1)
                probsT(1)
                square(2)
                outT(0)
                turned(2)
                square(3)
                turned(3)
                outT(1)
                exps(0)
                exps(1)
                values(0)
                values(1)
                if a:
                    g, _ = a
                    act.wait_ge(sem("d_xsT"), g + 1)
                    act.wait_ge(sem("d_vproj"), b[0] * 2 + 2 if b else g * 2)
                    nc.scalar.copy(xp[:, :], xcT[:, 0, :]).then_inc(sem("d_prev"), 1)
                if n:
                    g, _ = n
                    act.wait_ge(sem("d_xT"), g + 1)
                    act.wait_ge(sem("d_proj"), a[0] * 4 + 4 if a else g * 4)
                    if a:
                        act.wait_ge(sem("d_prev"), a[0] + 1)
                    nc.scalar.copy(xcT[0:64, 0, :], pt_[0:64, 0:P])
                    xv_ = xcT[64:P, 0, :].rearrange("p (b s) -> p b s", b=BT)
                    tv_ = pt_[64:P, 0:P].rearrange("p (b s) -> p b s", b=BT)
                    nc.scalar.copy(xv_[:, :, 1:S], tv_[:, :, 0:S - 1]).then_inc(sem("d_xsT"), 1)

            def f_body(a, b, c):
                def gelu(j):
                    if c:
                        g, _ = c
                        n = FBLK[j][1]
                        act.wait_ge(sem("f_h"), g * 3 + (j + 1))
                        act.wait_ge(sem("f_hT"), g * 3 + (j - 1 if j >= 2 else 0))
                        nc.scalar.activation(e[0:n, j % 2, 0:256], pj[j % 2][0:n, 0:256], ACT.Gelu, bias=fb1[0:n, 1, j:j + 1]).then_inc(sem("f_gl"), 1)

                gelu(0)
                gelu(1)
                if a:
                    g, _ = a
                    act.wait_ge(sem("f_sh"), g + 1)
                    nc.scalar.copy(xs[:, :, 64:128], pt_[:, 0:FT * 64].rearrange("p (a d) -> p a d", a=FT)).then_inc(sem("f_shc"), 1)
                gelu(2)
                if b:
                    g, _ = b
                    act.wait_ge(sem("f_xnT"), g + 1)
                    act.wait_ge(sem("f_h"), g * 3)
                    nc.scalar.activation(kT[:, 0:2, :].rearrange("p a t -> p (a t)"), pp[:, 0:2 * P], ACT.Identity, scale=fg[:, 0:1], bias=fg[:, 1:2]).then_inc(sem("f_xT"), 1)

            with act.Fori(0, DEPTH) as l:
                act.wait_ge(sem("f_h"), l * (3 * NF))
                act.wait_ge(sem("f_y"), l * NF)
                pipeline(act, NT, d_body, l * NT, 5)
                act.wait_ge(sem("d_s"), l * (2 * NT) + 2 * NT)
                act.wait_ge(sem("d_pt"), l * (2 * NT) + 2 * NT)
                act.wait_ge(sem("ffn_loaded"), l * FFN_LOADS + FFN_LOADS)
                pipeline(act, NF, f_body, l * NF, 3)

            def l_body(n, a, b, c, d):
                def exp1(g, h):
                    act.wait_ge(sem("l_sub"), g * 2 + (h + 1))
                    nc.scalar.activation(l_e1[h], l_e1[h], ACT.Exp, scale=L1D ** -0.5).then_inc(sem("l_e"), 1)

                def exp2(g, h):
                    act.wait_ge(sem("l_sub2"), g * 2 + (h + 1))
                    nc.scalar.activation(l_zb[h], l_zb[h], ACT.Exp).then_inc(sem("l_e2"), 1)

                def turned(g, h):
                    u = g * 2 + h
                    act.wait_ge(sem("l_pt"), u + 1)
                    reaches(act, "l_pv", u - 1)
                    nc.scalar.copy(pT[:, h, :], pp[:, :]).then_inc(sem("l_ptc"), 1)

                if a:
                    g, _ = a
                    act.wait_ge(sem("l_T"), g + 1)
                    reaches(act, "l_proj", g)
                    nc.scalar.copy(xcT[:, :, :].rearrange("p a t -> p (a t)"), pt_[:, 0:2 * P]).then_inc(sem("l_xcT"), 1)
                if d:
                    g, _ = d
                    act.wait_ge(sem("l_oT"), g + 1)
                    reaches(act, "l_pr", g)
                    nc.scalar.copy(oT[:, 0, :], po[0][:, 128:256]).then_inc(sem("l_oTc"), 1)
                if c:
                    g, t = c
                    reaches(act, "l_pv", g * 2)
                    past_waits(act, "act_went_on")
                    cv = CT[:, t, :].rearrange("p (b k d) -> p b k d", b=BT, d=L1D)
                    for par in range(2):
                        r = slice(par * 64, par * 64 + 64)
                        last = nc.scalar.copy(l_vp[r, :, :, par], cv[r])
                    last.then_inc(sem("l_Vc"), 1)
                    turned(g, 0)
                if b:
                    exp1(b[0], 0)
                if c:
                    exp2(c[0], 1)
                if a:
                    g, t = a
                    act.wait_ge(sem("l_proj"), g + 1)
                    past_waits(act, "act_went_on")
                    nc.scalar.copy(CT[:, t, :], pt_[:, 3 * P:4 * P]).then_inc(sem("l_V"), 1)
                if n:
                    g, t = n
                    reaches(act, "l_T", g)
                    past_waits(act, "act_went_on")
                    nc.scalar.copy(xs[:, 0, :], Y[:, t, :])
                    nc.scalar.copy(xs[:, 1, :], CT[:, t, :]).then_inc(sem("l_in"), 1)
                if b:
                    exp1(b[0], 1)
                if c:
                    turned(c[0], 1)
                if b:
                    exp2(b[0], 0)
                if a:
                    g, t = a
                    act.wait_ge(sem("l_gr"), g + 1)
                    past_waits(act, "act_went_on")
                    nc.scalar.copy(GR[:, t, :], pt_[:, 2 * P:2 * P + L1H]).then_inc(sem("l_grc"), 1)
                if c:
                    g, _ = c
                    act.wait_ge(sem("l_pv"), g * 2 + 2)
                    reaches(act, "l_oT", g)
                    nc.scalar.copy(tmp[:, :], po[0][:, 0:P]).then_inc(sem("l_o"), 1)

            act.wait_ge(sem("n_y"), 3)
            act.wait_ge(sem("zeroed"), 3)
            pipeline(act, NT, l_body, 0, 5)
            for i, some in enumerate(TURN4):
                act.wait_ge(sem("w_T"), i + 1)
                for j, (k, ex) in enumerate(some):
                    last = nc.scalar.copy(expert_T(k, ex), pt_[:, j * P:j * P + P])
                last.then_inc(sem("w_c"), 1)
            act.wait_ge(sem("g_T"), 1)
            nc.scalar.copy(egT[:, :], pp[:, 0:NE]).then_inc(sem("g_c"), 1)

            def r_body(a, b):
                if a:
                    g, t = a
                    act.wait_ge(sem("r_T"), g + 1)
                    act.wait_ge(sem("r_lg"), g)
                    nc.scalar.copy(xcT[:, 0, :], pt_[:, 0:P]).then_inc(sem("r_xT"), 1)
                    act.wait_ge(sem("r_xT"), g + 1)
                    past_waits(act, "act_went_on")
                    nc.scalar.copy(CT[:, t, :], xcT[:, 0, :]).then_inc(sem("r_XT"), 1)
                if b:
                    g, _ = b
                    act.wait_ge(sem("r_mx"), g + 1)
                    nc.scalar.activation(ss[:, 0, :], ss[:, 1, :], ACT.Exp, bias=mx[:, 0, 0:1], accum_out=sm[:, 0, 0:1]).then_inc(sem("r_e"), 1)

            pipeline(act, NT, r_body)

            with act.Fori(0, NM) as m:
                for ex in range(NEX):
                    act.wait_ge(sem("m_h"), m * NEX + (ex + 1))
                    act.wait_ge(sem("m_hT"), m * NEX + max(ex - 1, 0))
                    nc.scalar.activation(e[:, ex % 2, :], h_banks[ex % 2][0][:, :], ACT.Silu).then_inc(sem("m_silu"), 1)

        @block.vector
        def _(dve):
            def normalise(n, combine):
                with dve.Fori(0, NT // NB) as t:
                    if combine:
                        some = bass.ds(t * NB, NB)
                        nc.vector.scalar_tensor_tensor(X[:, some, :], Y[:, some, :], tg[:, 1:2], X[:, some, :], ALU.mult, ALU.add).then_inc(sem("n_x"), 1)
                        dve.wait_ge(sem("n_x"), t + 1)
                    for j in range(NB):
                        nc.vector.bn_stats(st[:, t * NB + j, :], X[:, t * NB + j, :]).then_inc(sem("n_st"), 1)
                dve.wait_ge(sem("n_st"), n * NT)
                nc.vector.tensor_tensor(mean[:, :], st[:, :, 1], st[:, :, 4], ALU.add)
                nc.vector.tensor_tensor(dif[:, :], st[:, :, 1], st[:, :, 4], ALU.subtract)
                nc.vector.tensor_tensor(m2[:, :], st[:, :, 2], st[:, :, 5], ALU.add).then_inc(sem("n_1"), 1)
                dve.wait_ge(sem("n_1"), n)
                nc.vector.tensor_scalar(mean[:, :], mean[:, :], 0.5, None, ALU.mult)
                nc.vector.scalar_tensor_tensor(dif[:, :], dif[:, :], 0.25, dif[:, :], ALU.mult, ALU.mult).then_inc(sem("n_2"), 1)
                dve.wait_ge(sem("n_2"), n)
                nc.vector.scalar_tensor_tensor(var[:, :], m2[:, :], 1.0 / D, dif[:, :], ALU.mult, ALU.add).then_inc(sem("n_var"), 1)
                dve.wait_ge(sem("n_rstd"), n)
                with dve.Fori(0, NT // NB) as t:
                    for j in range(NB):
                        k = t * NB + j
                        nc.vector.tensor_scalar(Y[:, k, :], X[:, k, :], mean[:, bass.ds(k, 1)], rstd[:, bass.ds(k, 1)], ALU.subtract, ALU.mult).then_inc(sem("y_ready" if n == 2 else "n_t"), 1)
                dve.wait_ge(sem("y_ready" if n == 2 else "n_t"), NT * (n if n == 1 else 1 if n == 2 else n - 1))
                nc.vector.tensor_copy(tmp[:, 0:1], mean[:, 0:1]).then_inc(sem("n_y"), 1)

            dve.wait_ge(s_ld, NLOAD)
            nc.vector.tensor_scalar(law[:, 1:2], law[:, 0:1], -1.0, 1.0, ALU.mult, ALU.add)
            dve.wait_ge(sem("tanh"), 1)
            normalise(1, False)
            dve.wait_ge(sem("zeroed"), 1)

            def x_body(a, b, c):
                def leave(tile, i):
                    g, _ = tile
                    dve.wait_ge(sem("x_proj"), g * 6 + (i + 1))
                    pv4 = pj[i % 2][:, :].rearrange("p (h t) -> p h t", h=4)
                    if i < 4:
                        hs = slice(4 * (i // 2), 4 * (i // 2) + 4)
                        if b:
                            dve.wait_ge(sem("x_s"), b[0] * 8 + (4 * (i // 2) + 4))
                        if i % 2 == 0:
                            for par in range(2):
                                r = slice(par * 64, par * 64 + 64)
                                last = nc.vector.tensor_tensor(qz[r, hs, par, :], pv4[r], bc(qb[r, hs], P), ALU.add)
                        else:
                            last = nc.vector.tensor_tensor(kT[:, hs, :], pv4, bc(kb[:, hs], P), ALU.add)
                    else:
                        reaches(dve, "x_pv", g * 8)
                        last = nc.vector.tensor_tensor(V[:, i - 4, :], pj[i % 2][:, :], vb[:, :, :].rearrange("p h d -> p (h d)"), ALU.add)
                    last.then_inc(sem("x_ev"), 1)

                def smax(k):
                    n = b[0] * 8 + (k + 1)
                    dve.wait_ge(sem("x_s"), n)
                    sv = sc[:, (k % 2) * 512:(k % 2) * 512 + 384].rearrange("p (a t) -> p a t", a=2)
                    nc.vector.tensor_reduce(mx[:, k % 2, 0:2], sv, AX, ALU.max).then_inc(sem("x_mx"), 1)
                    dve.wait_ge(sem("x_mx"), n)
                    reaches(dve, "x_pt", n - 4)
                    ev = e[:, k % 4, 0:384].rearrange("p (a t) -> p a t", a=2)
                    nc.vector.tensor_tensor(ev, sv, bc(mx[:, k % 2, 0:2], 192), ALU.subtract).then_inc(sem("x_sub"), 1)

                def sums(n, k):
                    dve.wait_ge(sem("x_e"), n)
                    reaches(dve, "x_p", n - 2)
                    ev = e[:, k % 4, 0:384].rearrange("p (a t) -> p a t", a=2)
                    nc.vector.tensor_reduce(sm[:, k % 2, 0:2], ev, AX, ALU.add).then_inc(sem("x_sum"), 1)
                    dve.wait_ge(sem("x_sum"), n)
                    nc.vector.reciprocal(rc[:, k % 2, 0:2], sm[:, k % 2, 0:2]).then_inc(sem("x_rc"), 1)

                for k in range(HP):
                    if b:
                        smax(k)
                    if k == 0:
                        if c:
                            sums(c[0] * 8 + 8, 7)
                    elif b:
                        sums(b[0] * 8 + k, k - 1)
                    if k == 2 and b:
                        leave(b, 4)
                        leave(b, 5)
                    if k == 4 and c:
                        g, t = c
                        dve.wait_ge(sem("x_wo"), g + 1)
                        nc.vector.tensor_tensor(tmp[:, :], po[1][:, 0:D], ob[:, :], ALU.add).then_inc(sem("x_tmp"), 1)
                        dve.wait_ge(sem("x_tmp"), g + 1)
                        nc.vector.scalar_tensor_tensor(X[:, t, :], tmp[:, :], tg[:, 0:1], X[:, t, :], ALU.mult, ALU.add).then_inc(sem("x_res"), 1)
                    if k in (4, 5) and a:
                        leave(a, k - 4)
                    if k == 7 and a:
                        leave(a, 2)
                        leave(a, 3)

            pipeline(dve, NT, x_body, 0, 3)
            dve.wait_ge(sem("x_res"), NT)
            normalise(2, False)

            def d_body(n, a, b, c, d):
                def rope(i):
                    if a:
                        g, _ = a
                        w = i // 2
                        dve.wait_ge(sem("d_sq"), g * 4 + (i + 1))
                        dve.wait_ge(sem("d_u"), g * 4 + (i - 1 if i >= 2 else 0))
                        if b:
                            dve.wait_ge(sem("d_qn" if i < 2 else "d_kn"), b[0] * 2 + (i % 2 + 1))
                        if i == 0:
                            dve.wait_ge(sem("d_xh"), g)
                        pv = pj[i % 2][:, :].rearrange("p (h d) -> p h d", d=DK)
                        t1v = U[i].rearrange("p (h d) -> p h d", d=DK)
                        t2v = t2b[i % 2].rearrange("p (h d) -> p h d", d=DK)

                        def table(tb, lo, hi):
                            return tb[:, w, lo:hi].unsqueeze(1).broadcast_to([P, 8, hi - lo])

                        nc.vector.tensor_tensor(t1v, pv, table(rc_, 0, DK), ALU.mult)
                        nc.vector.tensor_tensor(t2v[:, :, 0:32], pv[:, :, 32:64], table(rs_, 0, 32), ALU.mult)
                        nc.vector.tensor_tensor(t2v[:, :, 32:64], pv[:, :, 0:32], table(rs_, 32, 64), ALU.mult).then_inc(sem("d_rope"), 1)
                        nc.vector.tensor_reduce(ss[:, i, :], sqb[i % 2].rearrange("p (h d) -> p h d", d=DK), AX, ALU.add).then_inc(sem("d_ss"), 1)

                def newton_start():
                    if a:
                        g, _ = a
                        dve.wait_ge(sem("d_ss"), g * 4 + 4)
                        dve.wait_ge(sem("d_newton"), g * 12)
                        dve.wait_ge(sem("d_kn"), g * 2)
                        sv = ss[:, :, :].rearrange("p c h -> p (c h)")
                        nc.vector.tensor_scalar(ssc[:, :], sv, 1e-24, None, ALU.max).then_inc(sem("d_clamp"), 1)
                        nc.vector.tensor_scalar(xh[:, :], sv, 1e-24, -0.5, ALU.max, ALU.mult)
                        dve.wait_ge(sem("d_clamp"), g + 1)
                        nc.vector.tensor_scalar(ssc[:, :].bitcast(I32), ssc[:, :].bitcast(I32), 1, None, ALU.logical_shift_right).then_inc(sem("d_shift"), 1)
                        dve.wait_ge(sem("d_shift"), g + 1)
                        nc.vector.tensor_scalar(ny[:, 0, :].bitcast(I32), ssc[:, :].bitcast(I32), -1.0, float(0x5F3759DF), ALU.mult, ALU.add).then_inc(sem("d_xh"), 1)

                def unit(i):
                    if b:
                        g, _ = b
                        dve.wait_ge(sem("d_newton"), g * 12 + 12)
                        dve.wait_ge(sem("d_u"), g * 4 + (i + 1))
                        dve.wait_ge(sem("d_TT"), g * 4)
                        nc.vector.tensor_tensor(qn[:, i, :].rearrange("p (h d) -> p h d", d=DK),
                                                U[i].rearrange("p (h d) -> p h d", d=DK), bc(ny[:, 0, 8 * i:8 * i + 8], DK), ALU.mult).then_inc(sem("d_qn"), 1)

                def smax(h):
                    if b:
                        g, _ = b
                        dve.wait_ge(sem("d_s"), g * 2 + (h + 1))
                        sv = sc[:, h * 512:h * 512 + 512].rearrange("p (a t) -> p a t", t=S)
                        nc.vector.tensor_reduce(mx[:, h, 0:8], sv, AX, ALU.max).then_inc(sem("d_mx"), 1)
                        dve.wait_ge(sem("d_mx"), g * 2 + (h + 1))
                        dve.wait_ge(sem("d_pt"), g * 2)
                        nc.vector.tensor_tensor(e[:, h, :].rearrange("p (a t) -> p a t", t=S), sv, bc(mx[:, h, 0:8], S), ALU.subtract).then_inc(sem("d_sub"), 1)

                def sums(h):
                    if b:
                        g, _ = b
                        dve.wait_ge(sem("d_e"), g * 2 + (h + 1))
                        dve.wait_ge(sem("d_p"), g * 2)
                        nc.vector.tensor_reduce(sm[:, h, 0:8], e[:, h, :].rearrange("p (a t) -> p a t", t=S), AX, ALU.add).then_inc(sem("d_sum"), 1)
                        dve.wait_ge(sem("d_sum"), g * 2 + (h + 1))
                        nc.vector.reciprocal(rc[:, h, 0:8], sm[:, h, 0:8]).then_inc(sem("d_rc"), 1)

                unit(0)
                unit(1)
                if d:
                    g, t = d
                    dve.wait_ge(sem("d_wo"), g + 1)
                    nc.vector.tensor_tensor(Y[:, t, :], po[0][:, 256:256 + D], Y[:, t, :], ALU.add).then_inc(sem("d_res"), 1)
                rope(0)
                if n:
                    g, t = n
                    dve.wait_ge(sem("y_ready"), g + 1)
                    dve.wait_ge(sem("d_xT"), g)
                    nc.vector.tensor_copy(xs[:, 0, :], Y[:, t, :]).then_inc(sem("d_xin"), 1)
                rope(1)
                rope(2)
                rope(3)
                newton_start()
                smax(0)
                smax(1)
                sums(0)
                sums(1)

            def f_body(a, b, c):
                if b:
                    g, _ = b
                    dve.wait_ge(sem("f_rstd"), g + 1)
                    dve.wait_ge(sem("f_xnT"), g)
                    for i in range(FT):
                        last = nc.vector.tensor_scalar(qn[:, 0, 128 * i:128 * i + 128], xs[:, i, :], dif[:, 2 * i:2 * i + 1], rstd[:, i:i + 1], ALU.subtract, ALU.mult)
                    last.then_inc(sem("f_xn"), 1)
                if a:
                    g, t = a
                    dve.wait_ge(sem("d_res"), g * FT + FT)
                    dve.wait_ge(sem("f_xn"), (b or a)[0] + (1 if b else 0))
                    nc.vector.tensor_copy(xs[:, :, :], Y[:, bass.ds(t * FT, FT), :]).then_inc(sem("f_in"), 1)
                def gated(j):
                    if c:
                        g, _ = c
                        n = FBLK[j][1]
                        dve.wait_ge(sem("f_gl"), g * 3 + (j + 1))
                        dve.wait_ge(sem("f_y"), g)
                        nc.vector.scalar_tensor_tensor(big2[0:n, 256 * j:256 * j + 256], pj[j % 2][0:n, 256:512], fb1[0:n, 0, j:j + 1], e[0:n, j % 2, 0:256], ALU.add, ALU.mult).then_inc(sem("f_hT"), 1)

                gated(0)
                gated(1)
                if a:
                    g, _ = a
                    dve.wait_ge(sem("f_shc"), g + 1)
                    for i in range(FT):
                        last = nc.vector.bn_stats(st[:, i, :], xs[:, i, :])
                    last.then_inc(sem("f_st"), 1)
                gated(2)
                if a:
                    g, _ = a
                    dve.wait_ge(sem("f_st"), g + 1)
                    past_waits(dve, "dve_went_on")
                    for i in range(FT):
                        last = nc.vector.bn_aggr(dif[:, 2 * i:2 * i + 2], st[:, i, :])
                    last.then_inc(sem("f_ag"), 1)
                    dve.wait_ge(sem("f_ag"), g + 1)
                    dve.wait_ge(sem("f_eps"), g)
                    nc.vector.tensor_copy(var[:, 0:FT], dif[:, 1:2 * FT:2]).then_inc(sem("f_mv"), 1)
                if c:
                    g, t = c
                    dve.wait_ge(sem("f_y"), g + 1)
                    nc.vector.tensor_tensor(Y[:, bass.ds(t * FT, FT), :], sc[:, 0:2 * D].rearrange("p (a d) -> p a d", a=2), Y[:, bass.ds(t * FT, FT), :], ALU.add).then_inc(sem("y_ready"), FT)
                    nc.vector.tensor_copy(tmp[:, 1:2], fg[:, 1:2]).then_inc(sem("f_res"), 1)

            with dve.Fori(0, DEPTH) as l:
                dve.wait_ge(sem("att_loaded"), l * ATT_LOADS + ATT_LOADS)
                dve.wait_ge(sem("d_rope"), l * (NT * 4))
                for w, (cn, sn) in enumerate((("qcos", "qsin"), ("kcos", "ksin"))):
                    nc.vector.tensor_tensor(rc_[:, w, :], const(cn), qs[:, w, :], ALU.mult)
                    nc.vector.tensor_tensor(rs_[:, w, 0:32], const(sn)[:, 0:32], qs[:, w, 32:64], ALU.mult)
                    last = nc.vector.tensor_tensor(rs_[:, w, 32:64], const(sn)[:, 32:64], qs[:, w, 0:32], ALU.mult)
                last.then_inc(sem("tables"), 1)
                dve.wait_ge(sem("tables"), l + 1)
                dve.wait_ge(sem("f_xnT"), l * NF)
                dve.wait_ge(sem("f_shc"), l * NF)
                dve.wait_ge(sem("f_xn"), l * NF)
                pipeline(dve, NT, d_body, l * NT, 5)
                dve.wait_ge(sem("d_TT"), l * (4 * NT) + 4 * NT)
                dve.wait_ge(sem("d_xT"), l * NT + NT)
                dve.wait_ge(sem("ffn_loaded"), l * FFN_LOADS + FFN_LOADS)
                pipeline(dve, NF, f_body, l * NF, 3)
            dve.wait_ge(sem("f_res"), DEPTH * NF)
            dve.wait_ge(sem("y_ready"), NT * (DEPTH + 1))
            normalise(3, True)

            def l_body(n, a, b, c, d):
                def max1(g, h):
                    u = g * 2 + h
                    scv = sc[:, h * 512:h * 512 + 512].rearrange("p (j t) -> p j t", t=S)
                    dve.wait_ge(sem("l_s"), u + 1)
                    nc.vector.tensor_reduce(h8(mx, 0, h), scv, AX, ALU.max).then_inc(sem("l_mx"), 1)
                    dve.wait_ge(sem("l_mx"), u + 1)
                    reaches(dve, "l_m1", u - 1)
                    nc.vector.tensor_tensor(l_e1[h], scv, bc(h8(mx, 0, h), S), ALU.subtract).then_inc(sem("l_sub"), 1)

                def sum1(g, t, h):
                    u = g * 2 + h
                    dve.wait_ge(sem("l_e"), u + 1)
                    nc.vector.tensor_reduce(h8(sm, 0, h), l_e1[h], AX, ALU.add).then_inc(sem("l_sum"), 1)
                    dve.wait_ge(sem("l_sum"), u + 1)
                    nc.vector.reciprocal(h8(rc, 0, h), h8(sm, 0, h)).then_inc(sem("l_rc"), 1)
                    dve.wait_ge(sem("l_grc"), g + 1)
                    dve.wait_ge(sem("l_rc"), u + 1)
                    nc.vector.tensor_tensor(h8(rc, 1, h), GR[:, t, L1HALF * h:L1HALF * h + L1HALF], h8(rc, 0, h), ALU.mult)
                    nc.vector.tensor_scalar(h8(sm, 1, h), h8(rc, 0, h), law[:, 1:2], None, ALU.mult).then_inc(sem("l_c1"), 1)

                def max2(g, h):
                    u = g * 2 + h
                    dve.wait_ge(sem("l_z"), u + 1)
                    nc.vector.tensor_reduce(h8(mx, 1, h), l_zb[h], AX, ALU.max).then_inc(sem("l_mx2"), 1)
                    dve.wait_ge(sem("l_mx2"), u + 1)
                    nc.vector.tensor_tensor(l_zb[h], l_zb[h], bc(h8(mx, 1, h), S), ALU.subtract).then_inc(sem("l_sub2"), 1)

                def sum2(g, h):
                    u = g * 2 + h
                    s2, r2 = ssc[:, L1HALF * h:L1HALF * h + L1HALF], xh[:, L1HALF * h:L1HALF * h + L1HALF]
                    dve.wait_ge(sem("l_e2"), u + 1)
                    nc.vector.tensor_reduce(s2, l_zb[h], AX, ALU.add).then_inc(sem("l_sum2"), 1)
                    dve.wait_ge(sem("l_sum2"), u + 1)
                    nc.vector.reciprocal(r2, s2).then_inc(sem("l_rc2"), 1)
                    dve.wait_ge(sem("l_rc2"), u + 1)
                    nc.vector.scalar_tensor_tensor(l_zb[h], l_zb[h], law[:, 0:1], bc(r2, S), ALU.mult, ALU.mult).then_inc(sem("l_m2"), 1)

                if b:
                    max1(b[0], 0)
                if c:
                    max2(c[0], 1)
                if a:
                    g, _ = a
                    dve.wait_ge(sem("l_proj"), g + 1)
                    reaches(dve, "l_km", g)
                    nc.vector.tensor_copy(kT[:, 0, :], pj[0][:, P:2 * P]).then_inc(sem("l_kT"), 1)
                    reaches(dve, "l_s", g * 2)
                    nc.vector.tensor_copy(kT[:, 1, :], pj[0][:, 0:P]).then_inc(sem("l_qT"), 1)
                if d:
                    g, t = d
                    dve.wait_ge(sem("l_pr"), g + 1)
                    nc.vector.tensor_tensor(oT[:, 1, :], po[1][:, P:2 * P], lpb[:, :], ALU.add).then_inc(sem("l_tmp"), 1)
                if b:
                    sum1(*b, 0)
                if d:
                    g, t = d
                    dve.wait_ge(sem("l_tmp"), g + 1)
                    nc.vector.scalar_tensor_tensor(X[:, t, :], oT[:, 1, :], tg[:, 2:3], X[:, t, :], ALU.mult, ALU.add).then_inc(sem("l_res"), 1)
                if c:
                    sum2(c[0], 1)
                if a:
                    gv = pj[1][0:L1H, 0:P].rearrange("p (b t) -> p b t", b=BT)
                    nc.vector.tensor_reduce(l_gm[:, 0:2], gv, AX, ALU.max)
                    nc.vector.tensor_reduce(l_gm[:, 2:4], gv, AX, ALU.add).then_inc(sem("l_gm"), 1)
                if b:
                    max1(b[0], 1)
                if a:
                    g, _ = a
                    dve.wait_ge(sem("l_gm"), g + 1)
                    nc.vector.tensor_scalar(l_gm[:, 2:4], l_gm[:, 2:4], 0.5 / S, None, ALU.mult).then_inc(sem("l_g1"), 1)
                if a:
                    g, _ = a
                    dve.wait_ge(sem("l_g1"), g + 1)
                    nc.vector.scalar_tensor_tensor(l_gm[:, 4:6], l_gm[:, 0:2], 0.5, l_gm[:, 2:4], ALU.mult, ALU.add).then_inc(sem("l_g2"), 1)
                if a:
                    g, _ = a
                    dve.wait_ge(sem("l_g2"), g + 1)
                    reaches(dve, "l_gr", g)
                    nc.vector.tensor_copy(l_gb.rearrange("p (b s) -> p b s", b=BT), bc(l_gm[:, 4:6], S)).then_inc(sem("l_gb"), 1)
                if b:
                    max2(b[0], 0)
                    sum1(*b, 1)
                    sum2(b[0], 0)

            pipeline(dve, NT, l_body, 0, 5)
            dve.wait_ge(sem("l_res"), NT)
            normalise(4, False)

            idx = sb("idx", [P, 8], U32)
            idf = sb("idf", [P, 8])

            def r_body(a, b):
                if b:
                    g, t = b
                    lg = pp[:, 0:NE]
                    dve.wait_ge(sem("r_lg"), g + 1)
                    nc.vector.tensor_copy(ss[:, 1, :], lg)
                    nc.vector.tensor_reduce(mx[:, 0, 0:1], lg, AX, ALU.max, negate=True).then_inc(sem("r_mx"), 1)
                    dve.wait_ge(sem("r_e"), g + 1)
                    nc.vector.reciprocal(rc[:, 0, 0:1], sm[:, 0, 0:1]).then_inc(sem("r_rc"), 1)
                    dve.wait_ge(sem("r_rc"), g + 1)
                    nc.vector.tensor_scalar(ss[:, 2, :], ss[:, 0, :], rc[:, 0, 0:1], None, ALU.mult)
                    nc.vector.scalar_tensor_tensor(ss[:, 3, :], ss[:, 0, :], rc[:, 0, 0:1], egb[:, :], ALU.mult, ALU.add).then_inc(sem("r_sb"), 1)
                    dve.wait_ge(sem("r_sb"), g + 1)
                    nc.vector.tensor_copy(tmp[:, 0:1], law[:, 0:1])
                    nc.vector.max(rn[:, 0, :], ss[:, 3, :]).then_inc(sem("r_top"), 1)
                    dve.wait_ge(sem("r_top"), g + 1)
                    nc.vector.tensor_copy(tmp[:, 1:2], law[:, 0:1])
                    nc.vector.max_index(idx[:, :], rn[:, 0, :], ss[:, 3, :]).then_inc(sem("r_ix"), 1)
                    dve.wait_ge(sem("r_ix"), g + 1)
                    nc.vector.tensor_copy(idf[:, :], idx[:, :]).then_inc(sem("r_if"), 1)
                    dve.wait_ge(sem("r_if"), g + 1)
                    for i in range(2):
                        last = nc.vector.scalar_tensor_tensor(rn[:, 1 + i, :], const("iota"), idf[:, i:i + 1], ss[:, 2, :], ALU.is_equal, ALU.mult)
                    last.then_inc(sem("r_w"), 1)
                    dve.wait_ge(sem("r_w"), g + 1)
                    nc.vector.tensor_tensor(G[:, t, :], rn[:, 1, :], rn[:, 2, :], ALU.add).then_inc(sem("r_g"), 1)

            pipeline(dve, NT, r_body)

            acc = oT[:, 0:MT, :]
            with dve.Fori(0, NM) as m:
                def hidden(ex):
                    dve.wait_ge(sem("m_silu"), m * NEX + (ex + 1))
                    dve.wait_ge(sem("m_y"), m * NEX + max(ex - 1, 0))
                    nc.vector.tensor_tensor(pT[:, ex % 2, :], h_banks[ex % 2][1][:, :], e[:, ex % 2, :], ALU.mult).then_inc(sem("m_hT"), 1)

                hidden(0)
                for ex in range(NEX):
                    if ex + 1 < NEX:
                        hidden(ex + 1)
                    dve.wait_ge(sem("m_y"), m * NEX + (ex + 1))
                    yv = sc[:, (ex % 2) * 512:(ex % 2) * 512 + 512].rearrange("p (a d) -> p a d", a=MT)
                    gt = G[:, bass.ds(m * MT, MT), min(ex, NE - 1)]
                    if ex == 0:
                        nc.vector.tensor_tensor(acc, yv, bc(gt, D), ALU.mult).then_inc(sem("m_acc"), 1)
                        continue
                    av = qn[:, ex % 2, :].rearrange("p (a d) -> p a d", a=MT)
                    if ex < NE:
                        nc.vector.tensor_tensor(av, yv, bc(gt, D), ALU.mult).then_inc(sem("m_wy"), 1)
                        dve.wait_ge(sem("m_wy"), m * (NE - 1) + ex)
                    dve.wait_ge(sem("m_acc"), m * NEX + ex)
                    nc.vector.tensor_tensor(acc, av if ex < NE else yv, acc, ALU.add).then_inc(sem("m_acc"), 1)
                dve.wait_ge(sem("m_acc"), m * NEX + NEX)
                Xm = X[:, bass.ds(m * MT, MT), :]
                nc.vector.scalar_tensor_tensor(Xm, acc, tg[:, 3:4], Xm, ALU.mult, ALU.add).then_inc(sem("m_out"), 1)

        @block.tensor
        def _(pe):
            mm = nc.tensor.matmul
            pe.wait_ge(s_ld, NLOAD)
            for i in range(2):
                if i:
                    pe.wait_ge(sem("mk_c"), i)
                for j in range(4):
                    last = nc.tensor.transpose(pt_[:, j * P:j * P + P], mkn[:, (4 * i + j) * P:(4 * i + j + 1) * P], ident)
                last.then_inc(sem("mk_T"), 1)
            pe.wait_ge(sem("mk_c"), 2)

            def x_body(a, b, c):
                def scores(k):
                    g, _ = b
                    pe.wait_ge(sem("x_ev"), g * 6 + (2 if k < 4 else 4))
                    reaches(pe, "x_sub", g * 8 + (k - 1))
                    s0 = (k % 2) * 512
                    for par in range(2):
                        mm(sc[:, s0 + par * 256:s0 + par * 256 + MEM], qz[:, k, par, :], mkT[:, k, :], start=True, stop=True)
                    for par in range(2):
                        for bb in range(BT):
                            r = slice(bb * 64, bb * 64 + 64)
                            last = mm(sc[r, s0 + MEM + par * S:s0 + MEM + par * S + S], qz[:, k, par, r], kT[:, k, r], start=True, stop=True)
                    last.then_inc(sem("x_s"), 1)

                def turn(tile, k):
                    n = tile[0] * 8 + (k + 1)
                    pe.wait_ge(sem("x_p"), n)
                    reaches(pe, "x_ptc", n - 1)
                    for par in range(2):
                        nc.tensor.transpose(pp[:, par * P:par * P + P], e[:, k % 4, par * 256:par * 256 + MEM], ident)
                    nc.tensor.transpose(pp[:, 2 * P:3 * P], e[:, k % 4, MEM:MEM + 2 * S], ident).then_inc(sem("x_pt"), 1)

                def pv(tile, k):
                    g, _ = tile
                    pe.wait_ge(sem("x_ptc"), g * 8 + (k + 1))
                    if k == 0:
                        pe.wait_ge(sem("x_ev"), g * 6 + 6)
                    if k % 4 == 0:
                        reaches(pe, "x_o", g * 2 + k // 4)
                    c0 = (k % 4) * P
                    for par in range(2):
                        r = slice(par * 64, par * 64 + 64)
                        h0 = (2 * k + par) * DK
                        mm(po[0][r, c0:c0 + P], mvn[:, h0:h0 + DK], pT[:, k % 2, par * P:par * P + P], start=True, stop=False, skip_group_check=True)
                        for bb in range(BT):
                            last = mm(po[0][r, c0 + bb * 64:c0 + bb * 64 + 64], V[r, bb, k * DK:k * DK + DK],
                                      pT[r, k % 2, 2 * P + bb * 64:2 * P + bb * 64 + 64], start=False, stop=True, skip_group_check=True)
                    last.then_inc(sem("x_pv"), 1)

                def chunk(tile, i):
                    g, _ = tile
                    pe.wait_ge(sem("x_xcT"), g + 1)
                    reaches(pe, "x_ev", g * 6 + (i - 1))
                    for j in range(4 if i < 4 else 2):
                        if i < 4:
                            blk = (i // 2) * 4 + j
                            last = mm(pj[i % 2][:, j * P:j * P + P], (xk if i % 2 else xq)[:, blk * P:blk * P + P], xcT[:, i % 2, :], start=True, stop=True)
                        else:
                            bb = i - 4
                            last = mm(pj[i % 2][j * 64:j * 64 + 64, :], xcT[:, 1, bb * 64:bb * 64 + 64],
                                      xv[:, :].rearrange("p (h a d) -> p a h d", a=2, d=DK)[:, j], start=True, stop=True)
                    last.then_inc(sem("x_proj"), 1)

                for k in range(HP):
                    if b:
                        scores(k)
                    if k < 2:
                        if c:
                            turn(c, k + 6)
                    elif b:
                        turn(b, k - 2)
                    if k == 3:
                        if a:
                            g, _ = a
                            pe.wait_ge(sem("x_in"), g + 1)
                            reaches(pe, "x_xcT", g)
                            for i in range(2):
                                last = nc.tensor.transpose(pt_[:, i * P:i * P + P], xs[:, i, :], ident)
                            last.then_inc(sem("x_T"), 1)
                        if c:
                            g, _ = c
                            pe.wait_ge(sem("x_o"), g * 2 + 2)
                            reaches(pe, "x_res", g)
                            for i in range(HP):
                                last = mm(po[1][:, 0:D], oT[:, i, :], xo[:, i, :], start=(i == 0), stop=(i == HP - 1))
                            last.then_inc(sem("x_wo"), 1)
                    if k in (4, 5) and a:
                        chunk(a, k - 4)
                    if k == 7 and a:
                        chunk(a, 2)
                        chunk(a, 3)
                    if k < 3:
                        if c:
                            pv(c, k + 5)
                    elif b:
                        pv(b, k - 3)
                    if k == 2 and b:
                        chunk(b, 4)
                        chunk(b, 5)

            pipeline(pe, NT, x_body, 0, 3)
            pe.wait_ge(sem("cast"), 1)
            pe.wait_ge(sem("x_res"), NT)

            def d_body(n, a, b, c, d):
                def chunk(i):
                    if a:
                        g, _ = a
                        if i == 0:
                            pe.wait_ge(sem("d_xsT"), g + 1)
                        if i < 2:
                            pe.wait_ge(sem("d_v"), (b or a)[0] * 2)
                            if b:
                                pe.wait_ge(sem("d_rope"), b[0] * 4 + (i + 3))
                        else:
                            pe.wait_ge(sem("d_rope"), g * 4 + (i - 1))
                        mm(pj[i % 2][:, :], xcT[:, 0, :], wqkv[:, i * 512:i * 512 + 512], start=True, stop=True).then_inc(sem("d_proj"), 1)

                def values(i):
                    if b:
                        g, _ = b
                        pe.wait_ge(sem("d_prev"), g + 1)
                        pe.wait_ge(sem("d_rope"), a[0] * 4 + (i + 3) if a else g * 4 + 4)
                        mm(pj[i][:, :], xp[:, :], wqkv[:, (4 + i) * 512:(5 + i) * 512], start=True, stop=True).then_inc(sem("d_vproj"), 1)

                def turn(i):
                    if b:
                        g, _ = b
                        pe.wait_ge(sem("d_qn" if i < 2 else "d_kn"), g * 2 + (i % 2 + 1))
                        pe.wait_ge(sem("d_qkT"), g * 4 + i)
                        if i == 0 and a:
                            pe.wait_ge(sem("d_xsT"), a[0] + 1)
                        for j in range(4):
                            last = nc.tensor.transpose(pt_[:, j * P:j * P + P], qn[:, i, j * P:j * P + P], ident)
                        last.then_inc(sem("d_TT"), 1)

                def scores(h):
                    if b:
                        g, _ = b
                        if h == 0:
                            pe.wait_ge(sem("d_qkT"), g * 4 + 4)
                        pe.wait_ge(sem("d_sub"), g * 2)
                        mm(sc[:, h * 512:h * 512 + 512], identb[:, :], bandb[:, :, :, :].rearrange("p a b t -> p (a b t)"), start=True, stop=False, skip_group_check=True)
                        for j in range(4):
                            for bb in range(BT):
                                c0 = h * 512 + (j * BT + bb) * S
                                for par in range(2):
                                    r = slice(par * 64, par * 64 + 64)
                                    last = mm(sc[r, c0:c0 + S], qT[r, 4 * h + j, bb * 64:bb * 64 + 64], kT[r, 4 * h + j, bb * 64:bb * 64 + 64], start=False, stop=True, skip_group_check=True)
                        last.then_inc(sem("d_s"), 1)

                def probsT(h):
                    if c:
                        g, _ = c
                        pe.wait_ge(sem("d_p"), g * 2 + (h + 1))
                        pe.wait_ge(sem("d_ptc"), g * 2 + h)
                        for j in range(4):
                            last = nc.tensor.transpose(pp[:, j * P:j * P + P], e[:, h, j * P:j * P + P], ident)
                        last.then_inc(sem("d_pt"), 1)

                def pv(h):
                    if c:
                        g, _ = c
                        pe.wait_ge(sem("d_v"), g * 2 + 2)
                        pe.wait_ge(sem("d_ptc"), g * 2 + (h + 1))
                        pe.wait_ge(sem("d_o"), g * 2 + h)
                        pe.wait_ge(sem("d_res"), g)
                        past_waits(pe, "pe_went_on")
                        for j in range(4):
                            for par in range(2):
                                for bb in range(BT):
                                    r = slice(bb * 64, bb * 64 + 64)
                                    h0 = (2 * (4 * h + j) + par) * DK
                                    last = mm(po[bb][par * 64:par * 64 + 64, j * S:j * S + S],
                                              V[r, :, :].rearrange("p a c -> p (a c)")[:, h0:h0 + DK],
                                              pT[r, h, j * P + par * 64:j * P + par * 64 + 64], start=True, stop=True)
                        last.then_inc(sem("d_pv"), 1)

                chunk(0)
                chunk(1)
                turn(0)
                probsT(0)
                turn(1)
                probsT(1)
                chunk(2)
                pv(0)
                turn(2)
                chunk(3)
                turn(3)
                pv(1)
                scores(0)
                scores(1)
                values(0)
                values(1)
                if n:
                    g, _ = n
                    pe.wait_ge(sem("d_xin"), g + 1)
                    pe.wait_ge(sem("d_qkT"), b[0] * 4 + 4 if b else (a or n)[0] * 4)
                    nc.tensor.transpose(pt_[:, 0:P], xs[:, 0, :], ident).then_inc(sem("d_xT"), 1)
                if c:
                    g, _ = c
                    pe.wait_ge(sem("d_o"), g * 2 + 2)
                    for k in range(HP):
                        last = mm(po[0][:, 256:256 + D], oT[:, k, :], wo[:, k, :], start=(k == 0), stop=(k == HP - 1))
                    last.then_inc(sem("d_wo"), 1)

            def f_body(a, b, c):
                def hidden(j):
                    if c:
                        g, _ = c
                        o, n = FBLK[j]
                        if j == 0:
                            pe.wait_ge(sem("f_xT"), g + 1)
                        pe.wait_ge(sem("f_hT"), g * 3 + (j - 1 if j >= 2 else 0))
                        for k in (1, 0):
                            last = mm(pj[j % 2][0:n, (1 - k) * 256:(1 - k) * 256 + 256], fw1[:, k * FI + o:k * FI + o + n], kT[:, 0:2, :].rearrange("p a t -> p (a t)"), start=True, stop=True)
                        last.then_inc(sem("f_h"), 1)

                hidden(0)
                hidden(1)
                if a:
                    g, _ = a
                    pe.wait_ge(sem("f_in"), g + 1)
                    pe.wait_ge(sem("f_shc"), g)
                    mm(pt_[:, 0:FT * 64], const("shift"), xs[:, :, 64:128], start=True, stop=True).then_inc(sem("f_sh"), 1)
                if b:
                    g, _ = b
                    pe.wait_ge(sem("f_xn"), g + 1)
                    pe.wait_ge(sem("f_xT"), g)
                    for i in range(FT):
                        last = nc.tensor.transpose(pp[:, i * P:i * P + P], qn[:, 0, i * P:i * P + P], ident)
                    last.then_inc(sem("f_xnT"), 1)
                hidden(2)
                if c:
                    g, _ = c
                    pe.wait_ge(sem("y_ready"), g * FT + NT)
                    for i in range(FT):
                        mm(sc[:, i * D:i * D + D], const("ones")[0:1, :], fb2[:, :], start=True, stop=False)
                        for j, (o, n) in enumerate(FBLK):
                            if i == 0:
                                pe.wait_ge(sem("f_hT"), g * 3 + (j + 1))
                            last = mm(sc[:, i * D:i * D + D], big2[0:n, j * 256 + i * P:j * 256 + i * P + P], fw2[0:n, j, :], start=False, stop=(j == 2))
                    last.then_inc(sem("f_y"), 1)

            with pe.Fori(0, DEPTH) as l:
                pe.wait_ge(sem("att_loaded"), l * ATT_LOADS + ATT_LOADS)
                pe.wait_ge(sem("f_xT"), l * NF)
                pe.wait_ge(sem("f_shc"), l * NF)
                pe.wait_ge(sem("f_hT"), l * (3 * NF))
                pe.wait_ge(sem("y_ready"), l * NT + NT)
                pipeline(pe, NT, d_body, l * NT, 5)
                pe.wait_ge(sem("ffn_loaded"), l * FFN_LOADS + FFN_LOADS)
                pe.wait_ge(sem("d_v"), l * (2 * NT) + 2 * NT)
                pe.wait_ge(sem("d_qkT"), l * (4 * NT) + 4 * NT)
                pe.wait_ge(sem("d_ptc"), l * (2 * NT) + 2 * NT)
                pe.wait_ge(sem("d_sub"), l * (2 * NT) + 2 * NT)
                pipeline(pe, NF, f_body, l * NF, 3)

            def l_body(n, a, b, c, d):
                def turn(h):
                    if c:
                        u = c[0] * 2 + h
                        pe.wait_ge(sem("l_p"), u + 1)
                        reaches(pe, "l_ptc", u)
                        for j in range(4):
                            last = nc.tensor.transpose(pp[:, j * P:j * P + P], e[:, 2 + h, j * P:j * P + P], ident)
                        last.then_inc(sem("l_pt"), 1)

                def pv(h):
                    if c:
                        g, _ = c
                        pe.wait_ge(sem("l_ptc"), g * 2 + (h + 1))
                        pe.wait_ge(sem("l_Vc"), g + 1)
                        if h == 0:
                            reaches(pe, "l_res", g)
                        for k in range(4 * h, 4 * h + 4):
                            for bb in range(BT):
                                q = slice(bb * 64, bb * 64 + 64)
                                last = mm(po[0][q, 2 * k * L1D:2 * (k + 1) * L1D], pT[:, h, (k % 4) * P + bb * 64:(k % 4) * P + bb * 64 + 64],
                                          l_vp[:, bb, k], start=True, stop=True)
                        last.then_inc(sem("l_pv"), 1)

                def scores(h):
                    if a:
                        g, _ = a
                        pe.wait_ge(sem("l_km"), g + 1)
                        pe.wait_ge(sem("l_qT"), g + 1)
                        reaches(pe, "l_sub", g * 2 + (h - 1))
                        past_waits(pe, "pe_went_on")
                        r = slice(h * 64, h * 64 + 64)
                        for bb in range(BT):
                            q = slice(bb * 64, bb * 64 + 64)
                            last = mm(sc[q, h * 512:h * 512 + 512], kT[r, 1, q], l_km[r, bb], start=True, stop=True)
                        last.then_inc(sem("l_s"), 1)

                if a:
                    g, _ = a
                    pe.wait_ge(sem("l_in"), g + 1)
                    reaches(pe, "l_xcT", g)
                    reaches(pe, "l_grc", g)
                    for i in range(2):
                        last = nc.tensor.transpose(pt_[:, i * P:i * P + P], xs[:, i, :], ident)
                    last.then_inc(sem("l_T"), 1)
                if d:
                    pe.wait_ge(sem("l_o"), d[0] + 1)
                    nc.tensor.transpose(po[0][:, P:2 * P], tmp[:, :], ident).then_inc(sem("l_oT"), 1)
                turn(0)
                if a:
                    g, _ = a
                    pe.wait_ge(sem("l_xcT"), g + 1)
                    reaches(pe, "l_V", g)
                    reaches(pe, "l_kT", g)
                    reaches(pe, "l_qT", g)
                    reaches(pe, "l_gm", g)
                    mm(pj[0][:, P:2 * P], lkv[:, 0:D], xcT[:, 1, :], start=True, stop=True)
                    mm(pj[0][:, 0:P], lq[:, :], xcT[:, 0, :], start=True, stop=True)
                    mm(pj[1][0:L1H, 0:P], lla[:, :], xcT[:, 1, :], start=True, stop=True)
                    vv = lkv[:, D:2 * D].rearrange("p (h a d) -> p a h d", a=2, d=L1D)
                    for bb in range(BT):
                        for par in range(2):
                            last = mm(pt_[par * 64:par * 64 + 64, 3 * P + bb * 64:3 * P + bb * 64 + 64], xcT[:, 1, bb * 64:bb * 64 + 64], vv[:, par], start=True, stop=True)
                    last.then_inc(sem("l_proj"), 1)
                if d:
                    pe.wait_ge(sem("l_oTc"), d[0] + 1)
                    mm(po[1][:, P:2 * P], oT[:, 0, :], lpj[:, :], start=True, stop=True).then_inc(sem("l_pr"), 1)
                scores(0)
                pv(0)
                turn(1)
                pv(1)
                scores(1)
                if a:
                    g, _ = a
                    pe.wait_ge(sem("l_gb"), g + 1)
                    pe.wait_ge(sem("l_V"), g + 1)
                    mm(pt_[:, 2 * P:2 * P + L1H], l_gb, ident[0:L1H, 0:L1H], start=True, stop=True).then_inc(sem("l_gr"), 1)

            pe.wait_ge(sem("n_y"), 3)
            pipeline(pe, NT, l_body, 0, 5)
            pe.wait_ge(sem("exp_loaded"), 6 * 16)
            pe.wait_ge(sem("l_res"), NT)
            for i, some in enumerate(TURN4):
                if i:
                    pe.wait_ge(sem("w_c"), i)
                for j, (k, ex) in enumerate(some):
                    last = nc.tensor.transpose(pt_[:, j * P:j * P + P], expert_natural(k, ex), ident)
                last.then_inc(sem("w_T"), 1)
            nc.tensor.transpose(pp[:, 0:NE], egw[:, :], ident[0:NE, 0:NE]).then_inc(sem("g_T"), 1)
            pe.wait_ge(sem("g_c"), 1)
            pe.wait_ge(sem("w_c"), len(TURN4))

            def r_body(a, b):
                if a:
                    g, _ = a
                    pe.wait_ge(sem("r_in"), g + 1)
                    pe.wait_ge(sem("r_xT"), g)
                    nc.tensor.transpose(pt_[:, 0:P], xs[:, 0, :], ident).then_inc(sem("r_T"), 1)
                    pe.wait_ge(sem("r_XT"), g + 1)
                    pe.wait_ge(sem("r_mx"), g)
                    mm(pp[:, 0:NE], xcT[:, 0, :], egT[:, :], start=True, stop=True).then_inc(sem("r_lg"), 1)

            pipeline(pe, NT, r_body)

            pe.wait_ge(sem("r_g"), NT)
            with pe.Fori(0, NM) as m:
                def up(ex):
                    pe.wait_ge(sem("m_hT"), m * NEX + max(ex - 1, 0))
                    rows = CT[:, bass.ds(m * MT, MT), :].rearrange("p a t -> p (a t)")
                    mm(h_banks[ex % 2][0][:, :], expert_T(1, ex), rows, start=True, stop=True)
                    mm(h_banks[ex % 2][1][:, :], expert_T(3, ex), rows, start=True, stop=True).then_inc(sem("m_h"), 1)

                def down(ex):
                    pe.wait_ge(sem("m_hT"), m * NEX + (ex + 1))
                    pe.wait_ge(sem("m_acc"), m * NEX + (ex - 1 if ex >= 2 else 0))
                    for j in range(MT):
                        last = mm(sc[:, (ex % 2) * 512 + j * P:(ex % 2) * 512 + j * P + P], pT[:, ex % 2, j * P:j * P + P], expert_T(2, ex), start=True, stop=True)
                    last.then_inc(sem("m_y"), 1)

                up(0)
                for ex in range(NEX):
                    if ex + 1 < NEX:
                        up(ex + 1)
                    down(ex)


_INS = ['x', 'ctx_1024', 'g_xattn', 'g_ffn', 'L0_xattn_wq_w', 'L0_xattn_wq_b', 'L0_xattn_wk_w', 'L0_xattn_wk_b',
        'L0_xattn_wv_w', 'L0_xattn_wv_b', 'L0_xattn_mk', 'L0_xattn_mv', 'L0_xattn_wo_w', 'L0_xattn_wo_b',
        'L0_ffn_Wqkv', 'L0_ffn_q_scale', 'L0_ffn_k_scale', 'L0_ffn_Wo', 'L0_ffn_ln_g', 'L0_ffn_ln_b', 'L0_ffn_W1',
        'L0_ffn_b1', 'L0_ffn_W2', 'L0_ffn_b2', 'L1_xattn_w_kv', 'L1_xattn_w_q', 'L1_xattn_w_la', 'L1_xattn_w_proj',
        'L1_xattn_b_proj', 'L1_xattn_att_weight', 'L1_ffn_gate_w', 'L1_ffn_gate_bias', 'L1_ffn_w1', 'L1_ffn_w3',
        'L1_ffn_w2', 'L1_ffn_sw1', 'L1_ffn_sw3', 'L1_ffn_sw2']


def shape_constants():
    import numpy as np
    f = np.float32
    k = np.zeros((P, NCONST), f)

    def put(name, a):
        o, n = CONSTS[name]
        k[:, o:o + n] = a

    put("ident", np.eye(P, dtype=f))
    shift = np.zeros((P, P), f)
    for m in range(P):
        if m % S:
            shift[m - 1, m] = 1.0
    put("shift", shift)
    half = np.arange(0, DK, 2, dtype=f)
    inv_freq = f(1.0) / np.power(f(10000.0), half / f(DK))
    t = np.arange(S, dtype=f)
    freqs = np.concatenate([t[:, None] * inv_freq[None, :]] * 2, -1)
    base = (half + f(0.4 * DK)) / f(1.4 * DK)
    power = (t - S // 2) / f(WINDOW // 2)
    scale = np.concatenate([np.power(base[None, :], power[:, None])] * 2, -1)
    sign = np.where(np.arange(DK) < DK // 2, f(-1), f(1))
    for name, sc in (("q", scale), ("k", f(1.0) / scale)):
        put(name + "cos", np.tile(np.cos(freqs) * sc, (BT, 1)))
        put(name + "sin", np.tile(np.sin(freqs) * sc * sign, (BT, 1)))
    i, j = np.arange(S)[:, None], np.arange(S)[None, :]
    put("band", np.tile(np.where((i < j) | (i > j + WINDOW), f(MASKED), f(0)), (BT, 1)))
    put("iota", np.arange(NE, dtype=f)[None, :])
    put("headmask", (np.arange(P)[:, None] % 64 // L1D == np.arange(L1H // 2)[None, :]).astype(f))
    put("half", f(-0.5))
    put("eps", f(EPS))
    put("threehalves", f(1.5))
    put("ones", f(1.0))
    return k


def kernel(**inputs):
    import numpy as np
    import concourse.bacc as bacc
    from concourse.bass_utils import run_bass_kernel_spmd

    nc = bacc.Bacc("TRN2", target_bir_lowering=False, num_devices=1)
    arrays, args = {}, []
    for name in _INS + ["consts"]:
        a = shape_constants() if name == "consts" else np.ascontiguousarray(inputs[name])
        arrays[f"in_{name}"] = a
        args.append(nc.dram_tensor(f"in_{name}", a.shape, mybir.dt.from_np(a.dtype), kind="ExternalInput").ap())
    args.append(nc.dram_tensor("out_x", (B, S, D), F32, kind="ExternalOutput").ap())
    build(nc, *args)
    r = run_bass_kernel_spmd(nc, [arrays], core_ids=[0])
    return r.results[0]["out_x"]
```
